# Optimizing a Trainium2 kernel written in Bass

```python
import numpy as np
import jax
import jax.numpy as jnp

def _softmax(x, axis=-1):
    return jax.nn.softmax(x, axis=axis)

def _gelu(x):
    return jax.nn.gelu(x, approximate=True)

def _silu(x):
    return jax.nn.silu(x)

def _sigmoid(x):
    return jax.nn.sigmoid(x)

def _layernorm(x, axis=-1, eps=1e-05):
    m = jnp.mean(x, axis=axis, keepdims=True)
    v = jnp.var(x, axis=axis, keepdims=True)
    return (x - m) / jnp.sqrt(v + eps)

def _scatter_add(tgt, idx, src, axis=0):
    return tgt.at[idx].add(src)

def _segment_sum(src, seg, n):
    return jax.ops.segment_sum(src, seg, n)
kernel_name = 'mk_gnn_ffn_d2_gnn_r8_c8be57'

def setup_inputs(seed: int=0):
    np.random.seed(seed)
    _w = jnp.asarray

    def _rec_inputs():
        import jax
        import jax.numpy as jnp
        _gk = jax.random.key(seed)
        x = -0.0003713 + 1 * jax.random.normal(jax.random.fold_in(_gk, 1), (6250, 256), jnp.float32)
        src = jax.random.randint(jax.random.fold_in(_gk, 2), (100000,), 0, 6250, jnp.int32)
        dst = jax.random.randint(jax.random.fold_in(_gk, 3), (100000,), 0, 6250, jnp.int32)
        _o = jnp.argsort(dst, stable=True)
        src = src[_o]
        dst = dst[_o]
        edge_weight = jax.random.uniform(jax.random.fold_in(_gk, 12), (100000,), jnp.float32, 0.0, 0.999998)
        return (x, src, dst, edge_weight)
    x, src, dst, edge_weight = _rec_inputs()

    def _L0_gnn_setup():
        import jax, jax.numpy as jnp
        import numpy as np
        N = 6250
        E = 100000
        IN_DIM = 256
        HID_DIM = 64
        OUT_DIM = 256

        def _gcn_conv(x, src, dst, W, b, n_nodes):
            xw = x @ W
            ones = jnp.ones((src.shape[0],), dtype=x.dtype)
            deg = jax.ops.segment_sum(ones, dst, num_segments=n_nodes) + 1.0
            norm = jax.lax.rsqrt(deg)
            coef = (norm[src] * norm[dst])[:, None]
            msg = xw[src] * coef
            agg = jax.ops.segment_sum(msg, dst, num_segments=n_nodes)
            agg = agg + xw * (norm * norm)[:, None]
            return agg + b
        key = jax.random.key(seed)
        k_x, k_e, k_w1, k_b1, k_w2, k_b2 = jax.random.split(key, 6)
        x = jax.random.normal(k_x, (N, IN_DIM), dtype=jnp.float32)
        edge_index = jax.random.randint(k_e, (2, E), 0, N, dtype=jnp.int32)
        W1 = jax.random.normal(k_w1, (IN_DIM, HID_DIM), dtype=jnp.float32) * (1.0 / np.sqrt(IN_DIM))
        b1 = jnp.zeros((HID_DIM,), dtype=jnp.float32)
        W2 = jax.random.normal(k_w2, (HID_DIM, OUT_DIM), dtype=jnp.float32) * (1.0 / np.sqrt(HID_DIM))
        b2 = jnp.zeros((OUT_DIM,), dtype=jnp.float32)
        return {'x': x, 'edge_index': edge_index, 'W1': W1, 'b1': b1, 'W2': W2, 'b2': b2}
    _L0_gnn_all = _L0_gnn_setup()
    _L0_gnn_in = {k: v for k, v in _L0_gnn_all.items() if k in ('W1', 'b1', 'W2', 'b2')}
    del _L0_gnn_all

    def _L0_ffn_setup():
        import jax, jax.numpy as jnp
        import numpy as np
        TOP_K = 2
        LN_EPS = 1e-05
        key = jax.random.key(seed)
        ks = jax.random.split(key, 8)
        B, S, D, E, H = (16, 1024, 256, 8, 1024)
        x = jax.random.normal(ks[0], (B, S, D), dtype=jnp.float32)
        Wr = jax.random.normal(ks[1], (D, E), dtype=jnp.float32) * 0.1
        br = jnp.zeros((E,), dtype=jnp.float32)
        ln_g = jnp.ones((E, D), dtype=jnp.float32)
        ln_b = jnp.zeros((E, D), dtype=jnp.float32)
        W1 = jax.random.normal(ks[2], (E, D, H), dtype=jnp.float32) * (1.0 / np.sqrt(D))
        b1 = jnp.zeros((E, H), dtype=jnp.float32)
        W2 = jax.random.normal(ks[3], (E, H, D), dtype=jnp.float32) * (1.0 / np.sqrt(H))
        b2 = jnp.zeros((E, D), dtype=jnp.float32)
        return {'x': x, 'Wr': Wr, 'br': br, 'ln_g': ln_g, 'ln_b': ln_b, 'W1': W1, 'b1': b1, 'W2': W2, 'b2': b2}
    _L0_ffn_all = _L0_ffn_setup()
    _L0_ffn_in = {k: v for k, v in _L0_ffn_all.items() if k in ('Wr', 'br', 'ln_g', 'ln_b', 'W1', 'b1', 'W2', 'b2')}
    del _L0_ffn_all

    def _L1_gnn_setup():
        import jax, jax.numpy as jnp
        import numpy as np
        N_NODES = 6250
        N_EDGES = 100000
        IN_CH = 256
        OUT_CH = 256
        BN_EPS = 1e-05
        key = jax.random.key(seed)
        ks = jax.random.split(key, 5)
        x = jax.random.normal(ks[0], (N_NODES, IN_CH), dtype=jnp.float32)
        edge_index = jax.random.randint(ks[1], (2, N_EDGES), 0, N_NODES, dtype=jnp.int64)
        edge_attr = jax.random.uniform(ks[2], (N_EDGES,), dtype=jnp.float32)
        weight = jax.random.normal(ks[3], (IN_CH, OUT_CH), dtype=jnp.float32) / np.sqrt(IN_CH)
        bias = jnp.zeros((OUT_CH,), dtype=jnp.float32)
        bn_gamma = jnp.ones((OUT_CH,), dtype=jnp.float32)
        bn_beta = jnp.zeros((OUT_CH,), dtype=jnp.float32)
        return {'x': x, 'edge_attr': edge_attr, 'weight': weight, 'bias': bias, 'bn_gamma': bn_gamma, 'bn_beta': bn_beta, 'edge_index': edge_index}
    _L1_gnn_all = _L1_gnn_setup()
    _L1_gnn_in = {k: v for k, v in _L1_gnn_all.items() if k in ('weight', 'bias', 'bn_gamma', 'bn_beta')}
    del _L1_gnn_all

    def _L1_ffn_setup():
        import jax, jax.numpy as jnp
        import numpy as np
        B, K, D = (512, 16, 256)
        E = 32
        H = int(D * 0.25)
        key = jax.random.key(seed)
        ks = jax.random.split(key, 7)
        d_rs = D ** (-0.5)
        h_rs = H ** (-0.5)
        x = jax.random.normal(ks[0], (B, K, D), dtype=jnp.float32)
        router_w = jax.random.uniform(ks[1], (E, D), jnp.float32, -d_rs, d_rs)
        router_b = jax.random.uniform(ks[2], (E,), jnp.float32, -d_rs, d_rs)
        W1 = jax.random.uniform(ks[3], (E, D, H), jnp.float32, -h_rs, h_rs)
        b1 = jax.random.uniform(ks[4], (E, H), jnp.float32, -h_rs, h_rs)
        W2 = jax.random.uniform(ks[5], (E, H, D), jnp.float32, -d_rs, d_rs)
        b2 = jax.random.uniform(ks[6], (E, D), jnp.float32, -d_rs, d_rs)
        return {'x': x, 'router_w': router_w, 'router_b': router_b, 'W1': W1, 'b1': b1, 'W2': W2, 'b2': b2}
    _L1_ffn_all = _L1_ffn_setup()
    _L1_ffn_in = {k: v for k, v in _L1_ffn_all.items() if k in ('router_w', 'router_b', 'W1', 'b1', 'W2', 'b2')}
    del _L1_ffn_all
    return {'x': x, 'src': src, 'dst': dst, 'edge_weight': edge_weight, 'L0_gnn_W1': _L0_gnn_in['W1'], 'L0_gnn_b1': _L0_gnn_in['b1'], 'L0_gnn_W2': _L0_gnn_in['W2'], 'L0_gnn_b2': _L0_gnn_in['b2'], 'L0_ffn_Wr': _L0_ffn_in['Wr'], 'L0_ffn_br': _L0_ffn_in['br'], 'L0_ffn_ln_g': _L0_ffn_in['ln_g'], 'L0_ffn_ln_b': _L0_ffn_in['ln_b'], 'L0_ffn_W1': _L0_ffn_in['W1'], 'L0_ffn_b1': _L0_ffn_in['b1'], 'L0_ffn_W2': _L0_ffn_in['W2'], 'L0_ffn_b2': _L0_ffn_in['b2'], 'L1_gnn_weight': _L1_gnn_in['weight'], 'L1_gnn_bias': _L1_gnn_in['bias'], 'L1_gnn_bn_gamma': _L1_gnn_in['bn_gamma'], 'L1_gnn_bn_beta': _L1_gnn_in['bn_beta'], 'L1_ffn_router_w': _L1_ffn_in['router_w'], 'L1_ffn_router_b': _L1_ffn_in['router_b'], 'L1_ffn_W1': _L1_ffn_in['W1'], 'L1_ffn_b1': _L1_ffn_in['b1'], 'L1_ffn_W2': _L1_ffn_in['W2'], 'L1_ffn_b2': _L1_ffn_in['b2']}

def reference(x, src, dst, edge_weight, L0_gnn_W1, L0_gnn_b1, L0_gnn_W2, L0_gnn_b2, L0_ffn_Wr, L0_ffn_br, L0_ffn_ln_g, L0_ffn_ln_b, L0_ffn_W1, L0_ffn_b1, L0_ffn_W2, L0_ffn_b2, L1_gnn_weight, L1_gnn_bias, L1_gnn_bn_gamma, L1_gnn_bn_beta, L1_ffn_router_w, L1_ffn_router_b, L1_ffn_W1, L1_ffn_b1, L1_ffn_W2, L1_ffn_b2):
    import jax
    import jax.numpy as jnp

    def _L0_gnn_ref(x, edge_index, W1, b1, W2, b2):
        import jax, jax.numpy as jnp
        import numpy as np
        N = 6250
        E = 100000
        IN_DIM = 256
        HID_DIM = 64
        OUT_DIM = 256

        def _gcn_conv(x, src, dst, W, b, n_nodes):
            xw = x @ W
            ones = jnp.ones((src.shape[0],), dtype=x.dtype)
            deg = jax.ops.segment_sum(ones, dst, num_segments=n_nodes) + 1.0
            norm = jax.lax.rsqrt(deg)
            coef = (norm[src] * norm[dst])[:, None]
            msg = xw[src] * coef
            agg = jax.ops.segment_sum(msg, dst, num_segments=n_nodes)
            agg = agg + xw * (norm * norm)[:, None]
            return agg + b
        src, dst = (edge_index[0], edge_index[1])
        h = jax.nn.relu(_gcn_conv(x, src, dst, W1, b1, N))
        recon_x = _gcn_conv(h, src, dst, W2, b2, N)
        return recon_x

    def _L0_ffn_ref(x, Wr, br, ln_g, ln_b, W1, b1, W2, b2):
        import jax, jax.numpy as jnp
        import numpy as np
        TOP_K = 2
        LN_EPS = 1e-05
        B, S, D = x.shape
        N = B * S
        xt = x.reshape(N, D)
        logits = xt @ Wr + br
        probs = jax.nn.softmax(logits, axis=-1)
        top_p, top_idx = jax.lax.top_k(probs, TOP_K)
        weights = top_p / top_p.sum(axis=-1, keepdims=True)
        mu = xt.mean(axis=-1, keepdims=True)
        var = ((xt - mu) ** 2).mean(axis=-1, keepdims=True)
        xn = (xt - mu) * jax.lax.rsqrt(var + LN_EPS)
        xe = xn[None, :, :] * ln_g[:, None, :] + ln_b[:, None, :]
        h = jax.nn.gelu(jnp.einsum('end,edh->enh', xe, W1) + b1[:, None, :], approximate=False)
        y = jnp.einsum('enh,ehd->end', h, W2) + b2[:, None, :]
        y_tok = jnp.transpose(y, (1, 0, 2))
        sel = jnp.take_along_axis(y_tok, top_idx[:, :, None], axis=1)
        out = (weights[:, :, None] * sel).sum(axis=1)
        return out.reshape(B, S, D)

    def _L1_gnn_ref(x, edge_attr, weight, bias, bn_gamma, bn_beta, edge_index):
        import jax, jax.numpy as jnp
        import numpy as np
        N_NODES = 6250
        N_EDGES = 100000
        IN_CH = 256
        OUT_CH = 256
        BN_EPS = 1e-05
        n = x.shape[0]
        loop = jnp.arange(n, dtype=edge_index.dtype)
        src = jnp.concatenate([edge_index[0], loop])
        dst = jnp.concatenate([edge_index[1], loop])
        w = jnp.concatenate([edge_attr, jnp.ones((n,), x.dtype)])
        deg = jax.ops.segment_sum(w, dst, num_segments=n)
        dinv = jnp.where(deg > 0, jax.lax.rsqrt(deg), 0.0)
        norm = dinv[src] * w * dinv[dst]
        xw = x @ weight
        msgs = norm[:, None] * xw[src]
        agg = jax.ops.segment_sum(msgs, dst, num_segments=n) + bias
        mean = jnp.mean(agg, axis=0)
        var = jnp.mean(jnp.square(agg - mean), axis=0)
        y = (agg - mean) * jax.lax.rsqrt(var + BN_EPS) * bn_gamma + bn_beta
        return jax.nn.relu(y)

    def _L1_ffn_ref(x, router_w, router_b, W1, b1, W2, b2):
        import jax, jax.numpy as jnp
        import numpy as np
        B, K, D = (512, 16, 256)
        E = 32
        H = int(D * 0.25)
        xf = x.reshape(-1, D)
        logits = xf @ router_w.T + router_b
        idx = jnp.argmax(logits, axis=-1)
        w1t = jnp.take(W1, idx, axis=0)
        h = jnp.einsum('nd,ndh->nh', xf, w1t) + jnp.take(b1, idx, axis=0)
        h = jax.nn.relu(h)
        w2t = jnp.take(W2, idx, axis=0)
        out = jnp.einsum('nh,nhd->nd', h, w2t) + jnp.take(b2, idx, axis=0)
        out = jax.nn.relu(out)
        return out.reshape(x.shape)
    edge_index = jnp.stack([src, dst])
    x = x + _L0_gnn_ref(_layernorm(x, axis=-1), edge_index, L0_gnn_W1, L0_gnn_b1, L0_gnn_W2, L0_gnn_b2)
    x = x + _L0_ffn_ref(_layernorm(x, axis=-1)[None], L0_ffn_Wr, L0_ffn_br, L0_ffn_ln_g, L0_ffn_ln_b, L0_ffn_W1, L0_ffn_b1, L0_ffn_W2, L0_ffn_b2)[0]
    x = x + _L1_gnn_ref(_layernorm(x, axis=-1), edge_weight, L1_gnn_weight, L1_gnn_bias, L1_gnn_bn_gamma, L1_gnn_bn_beta, edge_index)
    x = x + _L1_ffn_ref(_layernorm(x, axis=-1)[None], L1_ffn_router_w, L1_ffn_router_b, L1_ffn_W1, L1_ffn_b1, L1_ffn_W2, L1_ffn_b2)[0]
    return x

_drawn_inputs = setup_inputs


def setup_inputs(seed=0):
    import zlib

    import numpy as np

    out = dict(_drawn_inputs(seed))
    spreads = {'L0_gnn_b1': (0.0, 0.1),
     'L0_gnn_b2': (0.0, 0.1),
     'L0_ffn_br': (0.0, 0.1),
     'L0_ffn_ln_g': (1.0, 0.2),
     'L0_ffn_ln_b': (0.0, 0.1),
     'L0_ffn_b1': (0.0, 0.1),
     'L0_ffn_b2': (0.0, 0.1),
     'L1_gnn_bias': (0.0, 0.8),
     'L1_gnn_bn_gamma': (1.0, 0.2),
     'L1_gnn_bn_beta': (0.0, 0.1)}
    factors = {'L1_ffn_b1': 8.0, 'L1_ffn_b2': 3.204}
    for name, (base, spread) in spreads.items():
        noise = np.random.default_rng([zlib.crc32(name.encode()), seed]).standard_normal(out[name].shape)
        drawn = base * np.exp(spread * noise) if base else spread * noise
        out[name] = jnp.asarray(drawn.astype(out[name].dtype))
    for name, factor in factors.items():
        out[name] = (out[name] * factor).astype(out[name].dtype)
    return out
```

```python
from contextlib import ExitStack

import concourse.bass as bass
from concourse import mybir

F32 = mybir.dt.float32
I32 = mybir.dt.int32
ALU = mybir.AluOpType
ACT = mybir.ActivationFunctionType
X = mybir.AxisListType.X

NODES, EDGES, DIM, HID = 6250, 100000, 256, 64
E0, H0, TOPK = 8, 1024, 2
E1, H1 = 32, 64
LN_EPS = BN_EPS = 1e-5

NB = 50
B = NODES // NB
ET = 125
NT = EDGES // ET
TP = 100
TG = NT // TP
U = 8
STEPS = -(-(NT + NB - 1) // (2 * U)) * 2 * U
SG = 8
SP = STEPS // SG
SPAD = STEPS + U
KC = DIM // 128
TT = 128
NT0 = -(-((TOPK * NODES + E0 * (TT - 1)) // TT) // 2) * 2
NT1 = -(-((NODES + E1 * (TT - 1)) // TT) // 2) * 2


class Parts:
    pass


def rep(ap, n):
    return ap.partition_broadcast(n)


def new(nc, ctx):
    taken = []

    def give_back():
        if taken:
            nc.clear_and_free_semaphores(taken)
            nc.all_engine_barrier()

    ctx.callback(give_back)

    def sb(name, shape, dt=F32):
        return ctx.enter_context(nc.sbuf_tensor(name, shape, dt))

    def ps(name):
        return ctx.enter_context(nc.psum_tensor(name, [128, 512], F32))

    def sem(name):
        taken.append(nc.alloc_semaphore(name))
        return taken[-1]

    return sb, ps, sem


def linker(eng, sem):
    count = [0]

    def link(ins):
        count[0] += 1
        ins.then_inc(sem, 1)
        eng.wait_ge(sem, count[0])

    return link


def schedule(nc, k, a):
    with ExitStack() as ctx:
        sb, ps, sem = new(nc, ctx)
        row_i = sb("row_i", [128, 128], I32)
        col_i = sb("col_i", [128, 1], I32)
        step_i = sb("step_i", [SP, SG], I32)
        step = sb("step", [SP, SG])
        dst_t = sb("dst_t", [TP, TG, ET], I32)
        ends = sb("ends", [TP, 2, TG])
        bound = sb("bound", [128, 2, NB])
        meets = sb("meets", [TP, 2, NB, TG])
        counts = sb("counts", [TP, 2, NB])
        below = sb("below", [128, 2, NB])
        ntile = sb("ntile", [128, NB])
        scan = sb("scan", [128, 2, NB])
        shift = sb("shift", [128, NB])
        cmp = sb("cmp", [SP, SG, NB])
        blk = sb("blk", [SP, SG])
        pick = sb("pick", [SP, SG, NB])
        off = sb("off", [SP, SG])
        tile_f = sb("tile_f", [SP, SG])
        tile_i = sb("tile_i", [SP, SG], I32)
        base = sb("base", [SP, SG])
        blk_f = sb("blk_f", [SP, SG])
        blk_i = sb("blk_i", [SP, SG], I32)
        rows_i = sb("rows_i", [SP, 2, SG, ET], I32)
        rows = sb("rows", [SP, 3, SG, ET])
        p_cnt = ps("p_cnt")
        p_rows = [ps(f"p_rows{n}") for n in range(6)]
        s_iota = sem("s_iota")
        s_load = sem("s_load")
        s_link = sem("s_link")
        s_counts = sem("s_counts")
        s_below = sem("s_below")
        s_tile = sem("s_tile")
        s_blk = sem("s_blk")
        s_blkst = sem("s_blkst")
        s_blkld = sem("s_blkld")
        s_rows = [sem(f"s_rows{n}") for n in range(3)]
        s_rowf = sem("s_rowf")
        s_rowT = sem("s_rowT")
        s_col = sem("s_col")
        block = ctx.enter_context(nc.Block())

        @block.sync
        def _(sp):
            sp.dma_start(dst_t[:, :, :], a["dst"].rearrange("(g p e) -> p g e", p=TP, e=ET)).then_inc(s_load, 16)
            sp.wait_ge(s_blk, 1)
            sp.dma_start(k.blk_dram.rearrange("(g p) -> p g", p=SP), blk_i[:, :],
                         allow_slow_non_contiguous=True).then_inc(s_blkst, 16)
            sp.wait_ge(s_blkst, 16)
            sp.dma_start(k.step_blk[0:1, :], k.blk_dram.rearrange("(o s) -> o s", o=1)).then_inc(s_blkld, 16)
            sp.wait_ge(s_blkld, 16)

        @block.gpsimd
        def _(pool):
            pool.iota(row_i[:, :], pattern=[[1, 128]], base=0, channel_multiplier=0).then_inc(s_iota, 1)
            pool.iota(col_i[:, :], pattern=[[1, 1]], base=0, channel_multiplier=1).then_inc(s_iota, 1)
            pool.iota(step_i[:, :], pattern=[[SP, SG]], base=0, channel_multiplier=1).then_inc(s_iota, 1)
            pool.wait_ge(s_tile, 1)
            for n, name in enumerate(("src", "dst", "edge_weight")):
                table = a[name].rearrange("(t e) -> t e", e=ET)
                for g in range(SG):
                    out = rows_i[:, n, g, :] if n < 2 else rows[:, 2, g, :]
                    pool.indirect_dma_start(
                        out=out, out_offset=None, in_=table,
                        in_offset=bass.IndirectOffsetOnAxis(ap=tile_i[:, g:g + 1], axis=0)).then_inc(s_rows[n], 16)

        @block.vector
        def _(dve):
            link = linker(dve, s_link)
            dve.memset(k.ones[:, :], 1.0)
            dve.memset(k.edge_ow[:, :, 0], 1.0)
            dve.memset(k.src_idx[:, STEPS:SPAD], 0)
            dve.memset(k.dst_rel[:, STEPS:SPAD], -1.0)
            dve.memset(k.edge_ow[:, STEPS:SPAD, 1], 0.0)
            dve.wait_ge(s_iota, 3)
            dve.tensor_copy(k.iota[:, :], row_i[:, :])
            dve.tensor_copy(step[:, :], step_i[:, :])
            link(dve.tensor_copy(k.col[:, :], col_i[:, :]))
            dve.tensor_scalar(k.ident[:, :], k.iota[:, :], k.col[:, 0:1], None, ALU.is_equal)
            dve.tensor_scalar(k.later[:, :], k.iota[:, :], k.col[:, 0:1], None, ALU.is_gt)
            dve.tensor_scalar(bound[:, 0, :], k.iota[:, 0:NB], float(B), None, ALU.mult)
            dve.tensor_scalar(bound[:, 1, :], k.iota[:, 0:NB], float(B), float(B), ALU.mult, ALU.add)
            dve.wait_ge(s_load, 16)
            dve.tensor_copy(ends[:, 0, :], dst_t[:, :, ET - 1])
            link(dve.tensor_copy(ends[:, 1, :], dst_t[:, :, 0]))
            for n in range(2):
                link(dve.tensor_tensor(meets[:, n, :, :], ends[:, n, :].unsqueeze(1).to_broadcast([TP, NB, TG]),
                                       bound[0:TP, n, :].unsqueeze(2).to_broadcast([TP, NB, TG]), ALU.is_lt))
            dve.tensor_reduce(counts[:, :, :], meets[:, :, :, :], X, ALU.add).then_inc(s_counts, 1)
            dve.wait_ge(s_below, 1)
            link(dve.tensor_copy(below[:, :, :].rearrange("p n b -> p (n b)"), p_cnt[:, 0:2 * NB]))
            link(dve.tensor_tensor(ntile[:, :], below[:, 1, :], below[:, 0, :], ALU.subtract))
            link(dve.tensor_copy(scan[:, 0, :], ntile[:, :]))
            d, at = 1, 0
            while d < NB:
                dve.tensor_copy(scan[:, 1 - at, 0:d], scan[:, at, 0:d])
                link(dve.tensor_tensor(scan[:, 1 - at, d:NB], scan[:, at, d:NB], scan[:, at, 0:NB - d], ALU.add))
                d, at = 2 * d, 1 - at
            ends_at = scan[:, at, :]
            link(dve.tensor_tensor(shift[:, :], below[:, 1, :], ends_at, ALU.subtract))
            link(dve.tensor_tensor(cmp[:, :, :], ends_at[0:SP].unsqueeze(1).to_broadcast([SP, SG, NB]),
                                   step[:, :].unsqueeze(2).to_broadcast([SP, SG, NB]), ALU.is_le))
            link(dve.tensor_reduce(blk[:, :], cmp[:, :, :], X, ALU.add))
            link(dve.tensor_tensor(pick[:, :, :], k.iota[0:SP, 0:NB].unsqueeze(1).to_broadcast([SP, SG, NB]),
                                   blk[:, :].unsqueeze(2).to_broadcast([SP, SG, NB]), ALU.is_equal))
            link(dve.tensor_tensor(cmp[:, :, :], pick[:, :, :],
                                   shift[0:SP, :].unsqueeze(1).to_broadcast([SP, SG, NB]), ALU.mult))
            link(dve.tensor_reduce(off[:, :], cmp[:, :, :], X, ALU.add))
            link(dve.tensor_tensor(tile_f[:, :], step[:, :], off[:, :], ALU.add))
            dve.tensor_scalar(tile_i[:, :], tile_f[:, :], float(NT - 1), 0.0, ALU.min, ALU.max).then_inc(s_tile, 1)
            dve.tensor_scalar(blk_i[:, :], blk[:, :], float(NB - 1), None, ALU.min).then_inc(s_blk, 1)
            link(dve.tensor_scalar(base[:, :], blk[:, :], float(B), None, ALU.mult))
            dve.wait_ge(s_rows[0], 16 * SG)
            dve.tensor_copy(rows[:, 0, :, :], rows_i[:, 0, :, :]).then_inc(s_rowf, 1)
            dve.wait_ge(s_rows[1], 16 * SG)
            link(dve.tensor_copy(rows[:, 1, :, :], rows_i[:, 1, :, :]))
            dve.tensor_tensor(rows[:, 1, :, :], rows[:, 1, :, :],
                              base[:, :].unsqueeze(2).to_broadcast([SP, SG, ET]), ALU.subtract).then_inc(s_rowf, 1)

        @block.tensor
        def _(pe):
            pe.wait_ge(s_counts, 1)
            pe.matmul(p_cnt[:, 0:2 * NB], k.ones[0:TP, :], counts[:, :, :].rearrange("p n b -> p (n b)"),
                      start=True, stop=True).then_inc(s_below, 1)
            for n in range(3):
                if n < 2:
                    pe.wait_ge(s_rowf, n + 1)
                else:
                    pe.wait_ge(s_rows[2], 16 * SG)
                for g in range(SG):
                    last = pe.transpose(p_rows[2 * n + g // 4][0:ET, (g % 4) * SP:(g % 4 + 1) * SP],
                                        rows[:, n, g, :], k.ident[0:SP, 0:SP])
                last.then_inc(s_rowT, 1)

        @block.scalar
        def _(act):
            for n, out in enumerate((k.src_idx, k.dst_rel, k.edge_ow[:, :, 1])):
                act.wait_ge(s_rowT, n + 1)
                for half in range(2):
                    act.copy(out[:, half * 4 * SP:(half + 1) * 4 * SP], p_rows[2 * n + half][0:ET, 0:4 * SP])


def rsqrt(link, dve, out, x, root, tmp):
    link(dve.reciprocal(out, root))
    link(dve.tensor_tensor(tmp, out, out, ALU.mult))
    link(dve.tensor_tensor(tmp, tmp, x, ALU.mult))
    link(dve.tensor_scalar(tmp, tmp, -0.5, 1.5, ALU.mult, ALU.add))
    link(dve.tensor_tensor(out, out, tmp, ALU.mult))


def rsqrt(link, dve, out, x, root, tmp):
    link(dve.reciprocal(out, root))
    link(dve.tensor_tensor(tmp, out, out, ALU.mult))
    link(dve.tensor_tensor(tmp, tmp, x, ALU.mult))
    link(dve.tensor_scalar(tmp, tmp, -0.5, 1.5, ALU.mult, ALU.add))
    link(dve.tensor_tensor(out, out, tmp, ALU.mult))


def degrees(nc, k, a):
    HALVES = STEPS // U
    with ExitStack() as ctx:
        sb, ps, sem = new(nc, ctx)
        sel = sb("sel_deg", [ET, 2, U, B])
        spread = sb("spread", [ET, 2, U, 2 * U])
        part = sb("part", [2 * U, HALVES, B])
        part_s = sb("part_s", [SP, SG, 2, B])
        in_blk = sb("in_blk", [SP, SG, NB])
        step_i = sb("step_i2", [SP, SG], I32)
        step_f = sb("step_f2", [SP, SG])
        degT = sb("degT", [NB, 2, B])
        deg = sb("deg", [B, 2, NB])
        live = sb("live", [B, 2, NB])
        root = sb("root", [B, 2, NB])
        tmp = sb("tmp_deg", [B, 2, NB])
        p_part = [ps(f"p_part{h}") for h in range(2)]
        p_deg, p_degT = ps("p_deg"), ps("p_degT")
        s_sel = [sem(f"s_dsel{h}") for h in range(2)]
        s_used = [sem(f"s_dused{h}") for h in range(2)]
        s_out = [sem(f"s_dout{h}") for h in range(2)]
        s_st, s_blk = sem("s_dst"), sem("s_dblk")
        s_in, s_deg, s_cp, s_T, s_root, s_link = (sem("s_d" + n) for n in ("in", "deg", "cp", "T", "root", "link"))
        block = ctx.enter_context(nc.Block())

        @block.vector
        def _(dve):
            link = linker(dve, s_link)
            link(dve.memset(spread[:, :, :, :].rearrange("p h u c -> p (h u c)"), 0.0))
            with dve.Fori(0, HALVES // 2) as i:
                for h in range(2):
                    dve.wait_ge(s_used[h], i)
                    for u in range(U):
                        m = h * U + u
                        dve.tensor_scalar(sel[:, h, u, :], k.iota[0:ET, 0:B], k.dst_rel[:, bass.ds(i * 2 * U + m, 1)],
                                          None, ALU.is_equal)
                        ins = dve.tensor_copy(spread[:, h, u, 2 * u:2 * u + 2],
                                              k.edge_ow[:, bass.ds(i * 2 * U + m, 1), :].rearrange("p o n -> p (o n)"))
                    ins.then_inc(s_sel[h], 1)
            dve.wait_ge(s_blk, 16)
            link(dve.tensor_copy(step_f[:, :], step_i[:, :]))
            dve.tensor_tensor(in_blk[:, :, :], k.iota[0:SP, 0:NB].unsqueeze(1).to_broadcast([SP, SG, NB]),
                              step_f[:, :].unsqueeze(2).to_broadcast([SP, SG, NB]), ALU.is_equal).then_inc(s_in, 1)
            dve.wait_ge(s_deg, 1)
            dve.tensor_copy(degT[:, :, :].rearrange("b n p -> b (n p)"), p_deg[0:NB, 0:2 * B]).then_inc(s_cp, 1)
            dve.wait_ge(s_T, 1)
            link(dve.tensor_scalar(deg[:, :, :].rearrange("p n b -> p (n b)"), p_degT[0:B, 0:2 * NB], 1.0, None, ALU.add))
            link(dve.tensor_scalar(live[:, :, :], deg[:, :, :], 0.0, None, ALU.is_gt))
            dve.tensor_scalar(deg[:, :, :], deg[:, :, :], 1e-30, None, ALU.max).then_inc(s_root, 1)
            dve.wait_ge(s_root, 2)
            rsqrt(link, dve, k.norm[:, :, :], deg[:, :, :], root[:, :, :], tmp[:, :, :])
            link(dve.tensor_tensor(k.norm[:, :, :], k.norm[:, :, :], live[:, :, :], ALU.mult))

        @block.scalar
        def _(act):
            with act.Fori(0, HALVES // 2) as i:
                for h in range(2):
                    act.wait_ge(s_used[h], i + 1)
                    act.copy(part[:, bass.ds(2 * i + h, 1), :].rearrange("p o b -> p (o b)"),
                             p_part[h][0:2 * U, 0:B]).then_inc(s_out[h], 1)
            act.wait_ge(s_root, 1)
            act.activation(root[:, :, :], deg[:, :, :], ACT.Sqrt).then_inc(s_root, 1)

        @block.sync
        def _(sp):
            sp.dma_start(step_i[:, :], k.blk_dram.rearrange("(g p) -> p g", p=SP),
                         allow_slow_non_contiguous=True).then_inc(s_blk, 16)
            for h in range(2):
                sp.wait_ge(s_out[h], HALVES // 2)
            sp.dma_start(k.part_dram.rearrange("(v u) (n b) -> (u n) v b", u=U, n=2), part[:, :, :]).then_inc(s_st, 16)
            sp.wait_ge(s_st, 16)
            sp.dma_start(part_s[:, :, :, :].rearrange("p g n b -> p g (n b)"),
                         k.part_dram.rearrange("(g p) c -> p g c", p=SP)).then_inc(s_st, 16)

        @block.tensor
        def _(pe):
            with pe.Fori(0, HALVES // 2) as i:
                for h in range(2):
                    pe.wait_ge(s_sel[h], i + 1)
                    pe.wait_ge(s_out[h], i)
                    for u in range(U):
                        ins = pe.matmul(p_part[h][0:2 * U, 0:B], spread[:, h, u, :], sel[:, h, u, :],
                                        start=(u == 0), stop=(u == U - 1))
                    ins.then_inc(s_used[h], 1)
            pe.wait_ge(s_st, 32)
            pe.wait_ge(s_in, 1)
            for g in range(SG):
                ins = pe.matmul(p_deg[0:NB, 0:2 * B], in_blk[:, g, :], part_s[:, g, :, :].rearrange("p n b -> p (n b)"),
                                start=(g == 0), stop=(g == SG - 1))
            ins.then_inc(s_deg, 1)
            pe.wait_ge(s_cp, 1)
            for n in range(2):
                ins = pe.transpose(p_degT[0:B, n * NB:(n + 1) * NB], degT[:, n, :], k.ident[0:NB, 0:NB])
            ins.then_inc(s_T, 1)


def stats_of(link, dve, s_root, stat, eps, mean, rstd, var, root, tmp):
    link(dve.tensor_tensor(mean, stat[:, :, 1], stat[:, :, 4], ALU.add))
    link(dve.tensor_tensor(tmp, stat[:, :, 1], stat[:, :, 4], ALU.subtract))
    link(dve.tensor_tensor(tmp, tmp, tmp, ALU.mult))
    link(dve.tensor_tensor(var, stat[:, :, 2], stat[:, :, 5], ALU.add))
    link(dve.tensor_scalar(mean, mean, 0.5, None, ALU.mult))
    link(dve.tensor_scalar(var, var, 1.0 / DIM, eps, ALU.mult, ALU.add))
    link(dve.scalar_tensor_tensor(var, tmp, 0.25, var, ALU.mult, ALU.add))
    ins = dve.tensor_scalar(var, var, 0.0, None, ALU.max)
    ins.then_inc(s_root, 1)
    dve.wait_ge(s_root, 2)
    rsqrt(link, dve, rstd, var, root, tmp)


def load_rows(nc, k, table, tag):
    CH = 5
    with ExitStack() as ctx:
        sb, ps, sem = new(nc, ctx)
        s_x = [sem(f"s_x{c}_{tag}") for c in range(CH)]
        block = ctx.enter_context(nc.Block())
        n = NB // CH

        @block.sync
        def _(sp):
            for c in range(CH):
                sp.dma_start(k.X[:, c * n:(c + 1) * n, :],
                             table.rearrange("(t p) d -> p t d", p=B)[:, c * n:(c + 1) * n, :]).then_inc(s_x[c], 16)

        @block.vector
        def _(dve):
            for c in range(CH):
                dve.wait_ge(s_x[c], 16)
                with dve.Fori(c * n, (c + 1) * n) as t:
                    dve.bn_stats(k.stat[:, bass.ds(t, 1), :].rearrange("p o s -> p (o s)"),
                                 k.X[:, bass.ds(t, 1), :].rearrange("p o d -> p (o d)"))


def project(nc, k, tag, weight, M, out, scale=None, keep=False):
    with ExitStack() as ctx:
        sb, ps, sem = new(nc, ctx)
        w = k.wrT if weight is None else sb("w_" + tag, [128, KC, M])
        mean, rstd, var, root, tmp = (sb(n + tag, [B, NB]) for n in ("mean", "rstd", "var", "root", "tmp"))
        z = sb("z_" + tag, [B, 2, DIM])
        zT = sb("zT_" + tag, [128, 2, KC, B])
        p_zT = [ps(f"p_zT{h}_{tag}") for h in range(2)]
        p_y = [ps(f"p_y{h}_{tag}") for h in range(2)]
        s_w, s_link, s_root = sem("s_w" + tag), sem("s_l" + tag), sem("s_r" + tag)
        s_z, s_T, s_c, s_mm, s_y = ([sem(f"s_{n}{h}_{tag}") for h in range(2)] for n in ("z", "T", "c", "mm", "y"))
        block = ctx.enter_context(nc.Block())

        if weight is not None:
            @block.sync
            def _(sp):
                sp.dma_start(w[:, :, :], weight).then_inc(s_w, 16)

        @block.vector
        def _(dve):
            link = linker(dve, s_link)
            stats_of(link, dve, s_root, k.stat, LN_EPS, mean[:, :], rstd[:, :], var[:, :], root[:, :], tmp[:, :])
            with dve.Fori(0, NB // 2) as i:
                for h in range(2):
                    x = k.X[:, bass.ds(2 * i + h, 1), :].rearrange("p o d -> p (o d)")
                    m, r = mean[:, bass.ds(2 * i + h, 1)], rstd[:, bass.ds(2 * i + h, 1)]
                    dve.wait_ge(s_T[h], i)
                    dve.tensor_scalar(z[:, h, :], x, m, r, ALU.subtract, ALU.mult).then_inc(s_z[h], 1)
                    if keep:
                        dve.tensor_scalar(x, x, m, r, ALU.subtract, ALU.mult)

        @block.tensor
        def _(pe):
            if weight is not None:
                pe.wait_ge(s_w, 16)
            with pe.Fori(0, NB // 2) as i:
                for h in range(2):
                    pe.wait_ge(s_z[h], i + 1)
                    pe.wait_ge(s_c[h], i)
                    for c in range(KC):
                        ins = pe.transpose(p_zT[h][:, c * B:(c + 1) * B], z[:, h, c * 128:(c + 1) * 128],
                                           k.ident[0:B, 0:B])
                    ins.then_inc(s_T[h], 1)
                for h in range(2):
                    pe.wait_ge(s_c[h], i + 1)
                    pe.wait_ge(s_y[h], i)
                    for c in range(KC):
                        ins = pe.matmul(p_y[h][0:B, 0:M], zT[:, h, c, :], w[:, c, :], start=(c == 0), stop=(c == KC - 1))
                    ins.then_inc(s_mm[h], 1)

        @block.scalar
        def _(act):
            act.wait_ge(s_root, 1)
            act.activation(root[:, :], var[:, :], ACT.Sqrt).then_inc(s_root, 1)
            with act.Fori(0, NB // 2) as i:
                for h in range(2):
                    act.wait_ge(s_T[h], i + 1)
                    act.wait_ge(s_mm[h], i)
                    act.copy(zT[:, h, :, :].rearrange("p c b -> p (c b)"), p_zT[h][:, 0:KC * B]).then_inc(s_c[h], 1)
                for h in range(2):
                    act.wait_ge(s_mm[h], i + 1)
                    o = out[:, bass.ds(2 * i + h, 1), :].rearrange("p o m -> p (o m)")
                    if scale is None:
                        act.copy(o, p_y[h][0:B, 0:M]).then_inc(s_y[h], 1)
                    else:
                        act.activation(o, p_y[h][0:B, 0:M], ACT.Copy,
                                       scale=scale[:, bass.ds(2 * i + h, 1)]).then_inc(s_y[h], 1)


def aggregate(nc, k, tag, table, D, acc, weighted):
    TURNS = STEPS // (2 * U)
    with ExitStack() as ctx:
        sb, ps, sem = new(nc, ctx)
        rows = sb("rows_" + tag, [ET, 2, U, D])
        idx = sb("idx_" + tag, [ET, 2, U], I32)
        sel = sb("sel_" + tag, [ET, 2, U, B])
        turn = sb("turn_" + tag, [1, 3])
        credit = sb("credit_" + tag, [1, 1])
        p_sum = [ps(f"p_sum{u}_{tag}") for u in range(U)]
        s_one, s_turn = sem("s_one" + tag), sem("s_turn" + tag)
        s_idx, s_rows, s_sel, s_sum, s_done = ([sem(f"s_{n}{h}_{tag}") for h in range(2)]
                                               for n in ("idx", "rows", "sel", "sum", "done"))
        block = ctx.enter_context(nc.Block())

        @block.scalar
        def _(act):
            with act.Fori(0, TURNS) as i:
                for h in range(2):
                    act.wait_ge(s_rows[h], i * U * 16)
                    act.copy(idx[:, h, :], k.src_idx[:, bass.ds(i * 2 * U + h * U, U)]).then_inc(s_idx[h], 1)

        @block.gpsimd
        def _(pool):
            pool.memset(turn[:, :], 0.0).then_inc(s_one, 1)
            pool.wait_ge(s_one, 1)
            with pool.Fori(0, TURNS) as i:
                for h in range(2):
                    pool.wait_ge(s_turn, 2 * i + h)
                    pool.wait_ge(s_idx[h], i + 1)
                    pool.wait_ge(s_sum[h], i * U)
                    pool.tensor_tensor(turn[:, 2:3], turn[:, 0:1], turn[:, 1:2], ALU.add).then_inc(s_turn, 1)
                    for u in range(U):
                        pool.indirect_dma_start(
                            out=rows[:, h, u, :], out_offset=None, in_=table,
                            in_offset=bass.IndirectOffsetOnAxis(ap=idx[:, h, u:u + 1], axis=0)).then_inc(s_rows[h], 16)

        @block.vector
        def _(dve):
            def select(h, at, turns):
                dve.wait_ge(s_sum[h], turns * U)
                for u in range(U):
                    w = k.edge_ow[:, bass.ds(at + u, 1), 1:2].rearrange("p a b -> p (a b)") if weighted else None
                    dve.tensor_scalar(sel[:, h, u, :], k.iota[0:ET, 0:B], k.dst_rel[:, bass.ds(at + u, 1)], w,
                                      ALU.is_equal, *([ALU.mult] if weighted else [])).then_inc(s_sel[h], 1)

            dve.memset(credit[:, :], 0.0).then_inc(s_done[1], U)
            for u in range(U):
                w = k.edge_ow[:, u, 1:2] if weighted else None
                dve.tensor_scalar(sel[:, 0, u, :], k.iota[0:ET, 0:B], k.dst_rel[:, u:u + 1], w,
                                  ALU.is_equal, *([ALU.mult] if weighted else [])).then_inc(s_sel[0], 1)
            with dve.Fori(0, TURNS) as i:
                for h in range(2):
                    select(1 - h, i * 2 * U + (h + 1) * U, i + h)
                    _, b = nc.values_load_multi_w_load_instructions(
                        k.step_blk[0:1, bass.ds(i * 2 * U + h * U, U)], engines=[mybir.EngineType.DVE],
                        min_val=0, max_val=NB - 1, skip_runtime_bounds_check_because="the schedule clamps it")
                    for u in range(U):
                        dve.wait_ge(s_sum[h], i * U + u + 1)
                        dve.wait_ge(s_done[h] if u else s_done[1 - h],
                                    i * U + u + h * U if u else i * U + U)
                        o = acc[:, bass.ds(b[u], 1), :].rearrange("p o d -> p (o d)")
                        dve.tensor_tensor(o, o, p_sum[u][0:B, 0:D], ALU.add).then_inc(s_done[h], 1)

        @block.tensor
        def _(pe):
            with pe.Fori(0, TURNS) as i:
                for h in range(2):
                    pe.wait_ge(s_rows[h], (i + 1) * U * 16)
                    for u in range(U):
                        pe.wait_ge(s_sel[h], i * U + u + 1)
                        pe.wait_ge(s_done[1 - h], i * U + u + 1)
                        pe.matmul(p_sum[u][0:B, 0:D], sel[:, h, u, :], rows[:, h, u, :],
                                  start=True, stop=True).then_inc(s_sum[h], 1)


def store_rows(nc, tag, src, table):
    with ExitStack() as ctx:
        s = new(nc, ctx)[2]("s_st" + tag)
        block = ctx.enter_context(nc.Block())

        @block.sync
        def _(sp):
            sp.dma_start(table.rearrange("(t p) d -> p t d", p=B), src).then_inc(s, 16)
            sp.wait_ge(s, 16)


def hidden(nc, k, a):
    with ExitStack() as ctx:
        sb, ps, sem = new(nc, ctx)
        b1 = sb("b1", [B, HID])
        s_b, s_link = sem("s_b1"), sem("s_hlink")
        block = ctx.enter_context(nc.Block())

        @block.sync
        def _(sp):
            sp.dma_start(b1[:, :], rep(a["L0_gnn_b1"], B)).then_inc(s_b, 16)

        @block.vector
        def _(dve):
            link = linker(dve, s_link)
            norm = k.norm[:, 0, :].unsqueeze(2).to_broadcast([B, NB, HID])
            acc = k.acc[:, :, :]
            link(dve.tensor_tensor(acc, acc, norm, ALU.mult))
            dve.wait_ge(s_b, 16)
            link(dve.tensor_tensor(acc, acc, b1[:, :].unsqueeze(1).to_broadcast([B, NB, HID]), ALU.add))
            link(dve.scalar_tensor_tensor(acc, acc, 0.0, norm, ALU.max, ALU.mult))


def conv_out(nc, k, a):
    with ExitStack() as ctx:
        sb, ps, sem = new(nc, ctx)
        w2 = sb("w2", [128, DIM])
        row = sb("row_w2", [B, 2, 128])
        rowT = sb("rowT_w2", [128, 2, B])
        p_T = [ps(f"p_T{h}_w2") for h in range(2)]
        p_y = [ps(f"p_y{h}_w2") for h in range(2)]
        s_w, s_x, s_one, s_st = sem("s_w_w2"), sem("s_x_w2"), sem("s_one_w2"), sem("s_st_w2")
        s_r, s_T, s_c, s_mm, s_y, s_bn = ([sem(f"s_{n}{h}_w2") for h in range(2)]
                                          for n in ("r", "T", "c", "mm", "y", "bn"))
        block = ctx.enter_context(nc.Block())

        @block.sync
        def _(sp):
            sp.wait_ge(s_one, 1)
            sp.dma_start(w2[0:HID, :], a["L0_gnn_W2"]).then_inc(s_w, 16)
            sp.dma_start(w2[HID:HID + 1, :], a["L0_gnn_b2"].rearrange("(o d) -> o d", o=1)).then_inc(s_w, 16)
            sp.dma_start(k.X[:, :, :], a["x"].rearrange("(t p) d -> p t d", p=B)).then_inc(s_x, 16)
            for h in range(2):
                sp.wait_ge(s_y[h], NB // 2)
            sp.dma_start(k.x1_dram.rearrange("(t p) d -> p t d", p=B), k.X[:, :, :]).then_inc(s_st, 16)
            sp.wait_ge(s_st, 16)

        @block.scalar
        def _(act):
            with act.Fori(0, NB // 2) as i:
                for h in range(2):
                    act.wait_ge(s_T[h], i)
                    act.activation(row[:, h, 0:HID], k.acc[:, bass.ds(2 * i + h, 1), :].rearrange("p o d -> p (o d)"),
                                   ACT.Copy, scale=k.norm[:, 0, bass.ds(2 * i + h, 1)]).then_inc(s_r[h], 1)
                for h in range(2):
                    act.wait_ge(s_T[h], i + 1)
                    act.wait_ge(s_mm[h], i)
                    act.copy(rowT[:, h, :], p_T[h][:, 0:B]).then_inc(s_c[h], 1)

        @block.tensor
        def _(pe):
            pe.wait_ge(s_w, 32)
            pe.wait_ge(s_one, 3)
            with pe.Fori(0, NB // 2) as i:
                for h in range(2):
                    pe.wait_ge(s_r[h], i + 1)
                    pe.wait_ge(s_c[h], i)
                    pe.transpose(p_T[h][:, 0:B], row[:, h, :], k.ident[0:B, 0:B]).then_inc(s_T[h], 1)
                for h in range(2):
                    pe.wait_ge(s_c[h], i + 1)
                    pe.wait_ge(s_y[h], i)
                    pe.matmul(p_y[h][0:B, 0:DIM], rowT[:, h, :], w2[:, :], start=True, stop=True).then_inc(s_mm[h], 1)

        @block.vector
        def _(dve):
            dve.memset(w2[:, :], 0.0).then_inc(s_one, 1)
            dve.memset(row[:, :, HID:HID + 1], 1.0).then_inc(s_one, 1)
            dve.memset(row[:, :, HID + 1:128], 0.0).then_inc(s_one, 1)
            dve.wait_ge(s_x, 16)
            with dve.Fori(0, NB // 2) as i:
                for h in range(2):
                    dve.wait_ge(s_mm[h], i + 1)
                    x = k.X[:, bass.ds(2 * i + h, 1), :].rearrange("p o d -> p (o d)")
                    dve.tensor_tensor(x, x, p_y[h][0:B, 0:DIM], ALU.add).then_inc(s_y[h], 1)
                for h in range(2):
                    dve.wait_ge(s_y[h], i + 1)
                    dve.bn_stats(k.stat[:, bass.ds(2 * i + h, 1), :].rearrange("p o s -> p (o s)"),
                                 k.X[:, bass.ds(2 * i + h, 1), :].rearrange("p o d -> p (o d)"))


def renormalise(nc, k):
    with ExitStack() as ctx:
        sb, ps, sem = new(nc, ctx)
        mean, rstd, var, root, tmp = (sb(n + "rn", [B, NB]) for n in ("mean", "rstd", "var", "root", "tmp"))
        s_link, s_root, s_stat = sem("s_lrn"), sem("s_rrn"), sem("s_srn")
        block = ctx.enter_context(nc.Block())

        @block.vector
        def _(dve):
            link = linker(dve, s_link)
            with dve.Fori(0, NB) as t:
                dve.bn_stats(k.stat[:, bass.ds(t, 1), :].rearrange("p o s -> p (o s)"),
                             k.X[:, bass.ds(t, 1), :].rearrange("p o d -> p (o d)")).then_inc(s_stat, 1)
            dve.wait_ge(s_stat, NB)
            stats_of(link, dve, s_root, k.stat, LN_EPS, mean[:, :], rstd[:, :], var[:, :], root[:, :], tmp[:, :])
            with dve.Fori(0, NB) as t:
                x = k.X[:, bass.ds(t, 1), :].rearrange("p o d -> p (o d)")
                dve.tensor_scalar(x, x, mean[:, bass.ds(t, 1)], rstd[:, bass.ds(t, 1)], ALU.subtract, ALU.mult)

        @block.scalar
        def _(act):
            act.wait_ge(s_root, 1)
            act.activation(root[:, :], var[:, :], ACT.Sqrt).then_inc(s_root, 1)


def route(nc, k, a, tag, E, top, bias, tiles):
    BE = NB * E
    G = -(-BE // 512)
    while BE % G:
        G += 1
    W = BE // G
    with ExitStack() as ctx:
        sb, ps, sem = new(nc, ctx)
        br = sb("br" + tag, [B, E])
        lg = sb("lg" + tag, [B, NB, E])
        cand = sb("cand" + tag, [B, NB, E])
        hot = sb("hot" + tag, [B, top, NB, E])
        mask = sb("mask" + tag, [B, NB, E])
        scan = sb("scan" + tag, [B, 2, NB, E])
        small = sb("small" + tag, [B, 4, NB])
        cnt = sb("cnt" + tag, [B, E])
        cnt_i = sb("cnt_i" + tag, [B, E], I32)
        til = sb("til" + tag, [B, E])
        tsc = sb("tsc" + tag, [B, 2, E])
        tcmp = sb("tcmp" + tag, [1, tiles + 2, E])
        tf = sb("tf" + tag, [1, tiles + 2])
        tio = sb("tio" + tag, [1, tiles + 2], I32)
        tiof = sb("tiof" + tag, [1, tiles + 2])
        p_rank = [ps(f"p_rank{g}_{tag}") for g in range(G)]
        p_tot = [ps(f"p_tot{g}_{tag}") for g in range(G)]
        s_b, s_link, s_e, s_m, s_p, s_io = (sem(f"s_{n}_{tag}") for n in ("b", "link", "e", "m", "p", "io"))
        block = ctx.enter_context(nc.Block())

        @block.sync
        def _(sp):
            sp.dma_start(br[:, :], rep(bias, B)).then_inc(s_b, 16)

        @block.gpsimd
        def _(pool):
            pool.iota(tio[:, :], pattern=[[1, tiles + 2]], base=0, channel_multiplier=0).then_inc(s_io, 1)

        @block.scalar
        def _(act):
            if top > 1:
                act.wait_ge(s_e, 1)
                act.activation(lg[:, :, :], lg[:, :, :], ACT.Exp).then_inc(s_e, 1)

        @block.tensor
        def _(pe):
            pe.wait_ge(s_m, 1)
            flat = mask[:, :, :].rearrange("p b e -> p (b e)")
            for g in range(G):
                pe.matmul(p_rank[g][0:B, 0:W], k.later[0:B, 0:B], flat[:, g * W:(g + 1) * W], start=True, stop=True)
                ins = pe.matmul(p_tot[g][0:B, 0:W], k.ones[0:B, 0:B], flat[:, g * W:(g + 1) * W], start=True, stop=True)
            ins.then_inc(s_p, 1)

        @block.vector
        def _(dve):
            link = linker(dve, s_link)
            wide = [B, NB, E]

            def per_node(n):
                return small[:, n, :].unsqueeze(2).to_broadcast(wide)

            def per_expert(x):
                return x.unsqueeze(1).to_broadcast(wide)

            dve.wait_ge(s_b, 16)
            link(dve.tensor_tensor(lg[:, :, :], k.logits[:, :, 0:E], per_expert(br[:, :]), ALU.add))
            if top > 1:
                link(dve.tensor_reduce(small[:, 0, :], lg[:, :, :], X, ALU.max))
                dve.tensor_tensor(lg[:, :, :], lg[:, :, :], per_node(0), ALU.subtract).then_inc(s_e, 1)
                dve.wait_ge(s_e, 2)
                link(dve.tensor_reduce(small[:, 0, :], lg[:, :, :], X, ALU.add))
                link(dve.reciprocal(small[:, 0, :], small[:, 0, :]))
                link(dve.tensor_tensor(lg[:, :, :], lg[:, :, :], per_node(0), ALU.mult))
            for n in range(top):
                link(dve.tensor_reduce(small[:, n, :], lg[:, :, :], X, ALU.max))
                link(dve.tensor_tensor(cand[:, :, :], lg[:, :, :], per_node(n), ALU.is_equal))
                link(dve.scalar_tensor_tensor(cand[:, :, :], cand[:, :, :], -64.0, per_expert(k.iota[0:B, 0:E]),
                                              ALU.mult, ALU.add))
                link(dve.tensor_reduce(small[:, 3, :], cand[:, :, :], X, ALU.min))
                link(dve.tensor_tensor(hot[:, n, :, :], cand[:, :, :], per_node(3), ALU.is_equal))
                if n + 1 < top:
                    link(dve.scalar_tensor_tensor(lg[:, :, :], hot[:, n, :, :], -2.0, lg[:, :, :], ALU.mult, ALU.add))
            if top > 1:
                link(dve.tensor_tensor(mask[:, :, :], hot[:, 0, :, :], hot[:, 1, :, :], ALU.add))
                link(dve.tensor_tensor(small[:, 2, :], small[:, 0, :], small[:, 1, :], ALU.add))
            else:
                link(dve.tensor_copy(mask[:, :, :], hot[:, 0, :, :]))
            dve.memset(tf[:, :], 0.0).then_inc(s_m, 1)
            if top > 1:
                link(dve.reciprocal(small[:, 2, :], small[:, 2, :]))
                for n in range(top):
                    dve.tensor_tensor(k.gate[:, n, :], small[:, n, :], small[:, 2, :], ALU.mult)
            dve.wait_ge(s_p, 1)
            for g in range(G):
                dve.tensor_copy(cand[:, :, :].rearrange("p b e -> p (b e)")[:, g * W:(g + 1) * W], p_rank[g][0:B, 0:W])
                link(dve.tensor_copy(scan[:, 0, :, :].rearrange("p b e -> p (b e)")[:, g * W:(g + 1) * W],
                                     p_tot[g][0:B, 0:W]))
            link(dve.tensor_tensor(cand[:, :, :], cand[:, :, :], scan[:, 0, :, :], ALU.subtract))
            d, at = 1, 0
            while d < NB:
                dve.tensor_copy(scan[:, 1 - at, 0:d, :], scan[:, at, 0:d, :])
                link(dve.tensor_tensor(scan[:, 1 - at, d:NB, :], scan[:, at, d:NB, :], scan[:, at, 0:NB - d, :], ALU.add))
                d, at = 2 * d, 1 - at
            link(dve.tensor_tensor(cand[:, :, :], cand[:, :, :], scan[:, at, :, :], ALU.add))
            link(dve.tensor_scalar(cnt[:, :], scan[:, at, NB - 1, :], float(TT - 1), None, ALU.add))
            link(dve.tensor_copy(cnt_i[:, :], cnt[:, :]))
            link(dve.tensor_scalar(cnt_i[:, :], cnt_i[:, :], TT.bit_length() - 1, None, ALU.logical_shift_right))
            link(dve.tensor_copy(til[:, :], cnt_i[:, :]))
            link(dve.tensor_copy(tsc[:, 0, :], til[:, :]))
            d, at = 1, 0
            while d < E:
                dve.tensor_copy(tsc[:, 1 - at, 0:d], tsc[:, at, 0:d])
                link(dve.tensor_tensor(tsc[:, 1 - at, d:E], tsc[:, at, d:E], tsc[:, at, 0:E - d], ALU.add))
                d, at = 2 * d, 1 - at
            ends = tsc[:, at, :]
            dve.wait_ge(s_io, 1)
            link(dve.tensor_copy(tiof[:, :], tio[:, :]))
            link(dve.tensor_tensor(tcmp[:, :, :], ends[0:1].unsqueeze(1).to_broadcast([1, tiles + 2, E]),
                                   tiof[:, :].unsqueeze(2).to_broadcast([1, tiles + 2, E]), ALU.is_le))
            link(dve.tensor_reduce(tf[:, :], tcmp[:, :, :], X, ALU.add))
            dve.tensor_scalar(k.tile_exp[0:1, 0:tiles + 2], tf[:, :], float(E - 1), None, ALU.min)
            link(dve.tensor_tensor(til[:, :], ends, til[:, :], ALU.subtract))
            link(dve.tensor_scalar(til[:, :], til[:, :], float(TT), None, ALU.mult))
            link(dve.tensor_tensor(cand[:, :, :], cand[:, :, :], per_expert(til[:, :]), ALU.add))
            for n in range(top):
                link(dve.tensor_tensor(hot[:, n, :, :], hot[:, n, :, :], cand[:, :, :], ALU.mult))
                link(dve.tensor_reduce(small[:, 3, :], hot[:, n, :, :], X, ALU.add))
                link(dve.tensor_copy(k.slot[:, n, :], small[:, 3, :]))


def dispatch(nc, k, tag, top):
    with ExitStack() as ctx:
        s = new(nc, ctx)[2]("s_disp" + tag)
        block = ctx.enter_context(nc.Block())

        @block.gpsimd
        def _(pool):
            for t in range(NB):
                for n in range(top):
                    pool.indirect_dma_start(
                        out=k.xg_dram, out_offset=bass.IndirectOffsetOnAxis(ap=k.slot[:, n, t:t + 1], axis=0),
                        in_=k.X[:, t, :], in_offset=None).then_inc(s, 16)
            pool.wait_ge(s, NB * top * 16)


def expert_bias(nc, k, a, w1, b1T):
    with ExitStack() as ctx:
        sb, ps, sem = new(nc, ctx)
        R = E0 * KC
        HC = H0 // 128
        rows = sb("gb_rows", [R, 2, 128])
        b1r = sb("b1_rows", [E0 * HC, 128])
        gb = sb("gb", [128, 2, R])
        b1c = sb("b1c", [128, E0 * HC])
        p_gb, p_b1, p_sh = ps("p_gb"), ps("p_b1"), ps("p_sh")
        s_ld, s_T, s_c, s_mm = sem("s_ebld"), sem("s_ebT"), sem("s_ebc"), sem("s_ebmm")
        s_w = [sem(f"s_ebw{c}") for c in range(KC)]
        block = ctx.enter_context(nc.Block())

        @block.sync
        def _(sp):
            sp.dma_start(rows[:, 0, :], a["L0_ffn_ln_g"].rearrange("e (c p) -> (e c) p", p=128)).then_inc(s_ld, 16)
            sp.dma_start(rows[:, 1, :], a["L0_ffn_ln_b"].rearrange("e (c p) -> (e c) p", p=128)).then_inc(s_ld, 16)
            sp.dma_start(b1r[:, :], a["L0_ffn_b1"].rearrange("e (c p) -> (e c) p", p=128)).then_inc(s_ld, 16)
            for c in range(KC):
                sp.dma_start(w1[:, c, :].rearrange("p (e h) -> p e h", e=E0),
                             a["L0_ffn_W1"].rearrange("e (c p) h -> c p e h", p=128)[c]).then_inc(s_w[c], 16)

        @block.tensor
        def _(pe):
            pe.wait_ge(s_ld, 48)
            for n in range(2):
                pe.transpose(p_gb[:, n * R:(n + 1) * R], rows[:, n, :], k.ident[0:R, 0:R])
            pe.transpose(p_b1[:, 0:E0 * HC], b1r[:, :], k.ident[0:E0 * HC, 0:E0 * HC]).then_inc(s_T, 1)
            pe.wait_ge(s_c, 1)
            for c in range(KC):
                pe.wait_ge(s_w[c], 16)
            for e in range(E0):
                for m in range(HC):
                    for c in range(KC):
                        ins = pe.matmul(p_sh[:, e * HC + m:e * HC + m + 1], w1[:, c, e * H0 + m * 128:e * H0 + (m + 1) * 128],
                                        gb[:, 1, e * KC + c:e * KC + c + 1], start=(c == 0), stop=(c == KC - 1))
                ins.then_inc(s_mm, 1)

        @block.vector
        def _(dve):
            dve.wait_ge(s_T, 1)
            dve.tensor_copy(b1c[:, :], p_b1[:, 0:E0 * HC])
            dve.tensor_copy(gb[:, :, :].rearrange("p n r -> p (n r)"), p_gb[:, 0:2 * R]).then_inc(s_c, 1)
            dve.wait_ge(s_c, 1)
            for e in range(E0):
                dve.wait_ge(s_mm, e + 1)
                for c in range(KC):
                    w = w1[:, c, e * H0:(e + 1) * H0]
                    dve.tensor_scalar(w, w, gb[:, 0, e * KC + c:e * KC + c + 1], None, ALU.mult)
            dve.tensor_tensor(b1T, b1c[:, :], p_sh[:, 0:E0 * HC], ALU.add)


def experts(nc, k, tag, tiles, E, H, w1, w2, b1T, b2, func):
    HC = -(-H // 128)
    HP = H // HC
    NW = min(H, 512)
    HB = H // NW
    with ExitStack() as ctx:
        sb, ps, sem = new(nc, ctx)
        x = sb("x" + tag, [TT, 2, DIM])
        xT = sb("xT" + tag, [128, 2, KC, TT])
        HW = max(H, 128)
        hid = sb("hid" + tag, [TT, 2, HW])
        hT = sb("hT" + tag, [HP, 2, HC, TT])
        y = sb("y" + tag, [TT, 2, DIM])
        p_x = ps("p_x" + tag)
        p_h = [[ps(f"p_h{h}{n}_{tag}") for n in range(HB)] for h in range(2)]
        TB = -(-HC // 4)
        p_t = [ps(f"p_t{n}_{tag}") for n in range(TB)]
        p_y = ps("p_y" + tag)
        s_x, s_xT, s_xc, s_h, s_hc, s_hT, s_g, s_mm, s_y, s_st = (
            [sem(f"s_{n}{h}_{tag}") for h in range(2)]
            for n in ("x", "xT", "xc", "h", "hc", "hT", "g", "mm", "y", "st"))
        block = ctx.enter_context(nc.Block())
        src = k.xg_dram.rearrange("(n p) d -> n p d", p=TT)
        dst = k.yg_dram.rearrange("(n p) d -> n p d", p=TT)
        PE, DVE, ACTE = mybir.EngineType.PE, mybir.EngineType.DVE, mybir.EngineType.Activation

        def expert_of(engine, at, n):
            return nc.values_load_multi_w_load_instructions(
                k.tile_exp[0:1, bass.ds(at, n)], engines=[engine], min_val=0, max_val=E - 1,
                skip_runtime_bounds_check_because="route clamps it")[1]

        @block.sync
        def _(sp):
            for h in range(2):
                sp.dma_start(x[:, h, :], src[h]).then_inc(s_x[h], 16)
            with sp.Fori(0, tiles // 2) as i:
                for h in range(2):
                    sp.wait_ge(s_xT[h], i + 1)
                    sp.dma_start(x[:, h, :], src[bass.ds(2 * i + 2 + h, 1)].rearrange("o p d -> (o p) d")).then_inc(s_x[h], 16)
                    sp.wait_ge(s_y[h], i + 1)
                    sp.dma_start(dst[bass.ds(2 * i + h, 1)].rearrange("o p d -> (o p) d"), y[:, h, :]).then_inc(s_st[h], 16)
            for h in range(2):
                sp.wait_ge(s_st[h], tiles // 2 * 16)
                sp.wait_ge(s_x[h], (tiles // 2 + 1) * 16)

        @block.tensor
        def _(pe):
            def turn_x(h, turns):
                pe.wait_ge(s_x[h], (turns + 1) * 16)
                pe.wait_ge(s_xc[1 - h], turns + h)
                for c in range(KC):
                    ins = pe.transpose(p_x[:, c * TT:(c + 1) * TT], x[:, h, c * 128:(c + 1) * 128], k.ident[:, :])
                ins.then_inc(s_xT[h], 1)

            def up(h, turns, e):
                pe.wait_ge(s_xc[h], turns + 1)
                pe.wait_ge(s_hc[h], turns)
                for n in range(HB):
                    for c in range(KC):
                        ins = pe.matmul(p_h[h][n][:, 0:NW], xT[:, h, c, :],
                                        w1[:, c, bass.ds(e * H + n * NW, NW)], start=(c == 0), stop=(c == KC - 1))
                ins.then_inc(s_h[h], 1)

            def turn_h(h, turns):
                pe.wait_ge(s_hc[h], turns + 1)
                pe.wait_ge(s_g[1 - h], turns + h)
                for m in range(HC):
                    ins = pe.transpose(p_t[m // 4][:, (m % 4) * TT:(m % 4 + 1) * TT], hid[:, h, m * 128:(m + 1) * 128],
                                       k.ident[:, :])
                ins.then_inc(s_hT[h], 1)

            def down(h, turns, e):
                pe.wait_ge(s_g[h], turns + 1)
                pe.wait_ge(s_y[1 - h], turns + h)
                for m in range(HC):
                    ins = pe.matmul(p_y[:, 0:DIM], hT[:, h, m, :], w2[:, m, bass.ds(e * DIM, DIM)],
                                    start=(m == 0), stop=(m == HC - 1))
                ins.then_inc(s_mm[h], 1)

            turn_x(0, 0)
            (e,) = expert_of(PE, 0, 1)
            up(0, 0, e)
            turn_x(1, 0)
            with pe.Fori(0, tiles // 2) as i:
                e = expert_of(PE, 2 * i, 3)
                for h in range(2):
                    turn_h(h, i)
                    up(1 - h, i + h, e[h + 1])
                    turn_x(h, i + 1)
                    down(h, i, e[h])

        @block.scalar
        def _(act):
            def copy_x(h, turns):
                act.wait_ge(s_xT[h], turns + 1)
                act.wait_ge(s_h[h], turns)
                act.copy(xT[:, h, :, :].rearrange("p c t -> p (c t)"), p_x[:, 0:KC * TT]).then_inc(s_xc[h], 1)

            copy_x(0, 0)
            copy_x(1, 0)
            with act.Fori(0, tiles // 2) as i:
                e = expert_of(ACTE, 2 * i, 2)
                for h in range(2):
                    act.wait_ge(s_hT[h], i + 1)
                    act.wait_ge(s_mm[h], i)
                    for m in range(HC):
                        ins = act.activation(hT[:, h, m, :], p_t[m // 4][0:HP, (m % 4) * TT:(m % 4 + 1) * TT], func,
                                             bias=b1T[0:HP, bass.ds(e[h] * HC + m, 1)])
                    ins.then_inc(s_g[h], 1)
                    copy_x(h, i + 1)

        @block.vector
        def _(dve):
            def copy_h(h, turns):
                dve.wait_ge(s_h[h], turns + 1)
                dve.wait_ge(s_hT[h], turns)
                for n in range(HB):
                    ins = dve.tensor_copy(hid[:, h, n * NW:(n + 1) * NW], p_h[h][n][:, 0:NW])
                ins.then_inc(s_hc[h], 1)

            if H < HW:
                dve.memset(hid[:, :, H:HW], 0.0)
            copy_h(0, 0)
            with dve.Fori(0, tiles // 2) as i:
                e = expert_of(DVE, 2 * i, 2)
                for h in range(2):
                    copy_h(1 - h, i + h)
                    dve.wait_ge(s_mm[h], i + 1)
                    dve.wait_ge(s_st[h], i * 16)
                    dve.tensor_tensor(y[:, h, :], p_y[:, 0:DIM], b2[:, bass.ds(e[h] * DIM, DIM)], ALU.add).then_inc(s_y[h], 1)


def first_ffn(nc, k, a):
    HC = H0 // 128
    with ExitStack() as scope:
        sb, ps, sem = new(nc, scope)
        w1 = sb("ffn0_w1", [128, KC, E0 * H0])
        w2 = sb("ffn0_w2", [128, HC, E0 * DIM])
        b1T = sb("ffn0_b1T", [128, E0 * HC])
        b2 = sb("ffn0_b2", [128, E0 * DIM])
        expert_bias(nc, k, a, w1, b1T[:, :])
        with ExitStack() as ctx:
            s_w = new(nc, ctx)[2]("s_w2ld")
            block = ctx.enter_context(nc.Block())

            @block.sync
            def _(sp):
                for m in range(HC):
                    sp.dma_start(w2[:, m, :].rearrange("p (e d) -> p e d", e=E0),
                                 a["L0_ffn_W2"].rearrange("e (m p) d -> m p e d", p=128)[m]).then_inc(s_w, 16)
                sp.dma_start(b2[:, :], rep(a["L0_ffn_b2"].rearrange("e d -> (e d)"), 128)).then_inc(s_w, 16)
                sp.wait_ge(s_w, 16 * (HC + 1))
        experts(nc, k, "f0", NT0, E0, H0, w1, w2, b1T, b2, ACT.Gelu)


def second_ffn(nc, k, a):
    with ExitStack() as scope:
        sb, ps, sem = new(nc, scope)
        w1 = sb("ffn1_w1", [128, KC, E1 * H1])
        w2 = sb("ffn1_w2", [H1, 1, E1 * DIM])
        b1r = sb("ffn1_b1r", [E1, H1])
        b1T = sb("ffn1_b1T", [H1, E1])
        b2 = sb("ffn1_b2", [128, E1 * DIM])
        with ExitStack() as ctx:
            _, ps2, _ = new(nc, ctx)
            p_b = ps2("p_b1T")
            s_w = new(nc, ctx)[2]("s_w1ld")
            s_b = new(nc, ctx)[2]("s_b1ld")
            s_T = new(nc, ctx)[2]("s_b1T")
            block = ctx.enter_context(nc.Block())

            @block.sync
            def _(sp):
                sp.dma_start(b1r[:, :], a["L1_ffn_b1"]).then_inc(s_b, 16)
                for c in range(KC):
                    sp.dma_start(w1[:, c, :].rearrange("p (e h) -> p e h", e=E1),
                                 a["L1_ffn_W1"].rearrange("e (c p) h -> c p e h", p=128)[c]).then_inc(s_w, 16)
                sp.dma_start(w2[:, 0, :].rearrange("p (e d) -> p e d", e=E1),
                             a["L1_ffn_W2"].rearrange("e p d -> p e d")).then_inc(s_w, 16)
                sp.dma_start(b2[:, :], rep(a["L1_ffn_b2"].rearrange("e d -> (e d)"), 128)).then_inc(s_w, 16)
                sp.wait_ge(s_w, 16 * (KC + 2))

            @block.tensor
            def _(pe):
                pe.wait_ge(s_b, 16)
                pe.transpose(p_b[0:H1, 0:E1], b1r[:, :], k.ident[0:E1, 0:E1]).then_inc(s_T, 1)

            @block.vector
            def _(dve):
                dve.wait_ge(s_T, 1)
                dve.tensor_copy(b1T[:, :], p_b[0:H1, 0:E1])
        experts(nc, k, "f1", NT1, E1, H1, w1, w2, b1T, b2, ACT.Relu)


def combine(nc, k, tag, table, top, out, relu=False):
    R = 8
    with ExitStack() as ctx:
        sb, ps, sem = new(nc, ctx)
        got = sb("got" + tag, [B, R, top, DIM])
        s_x, s_o = sem("s_x" + tag), sem("s_o" + tag)
        s_got = [sem(f"s_got{r}_{tag}") for r in range(R)]
        s_used = sem("s_used" + tag)
        s_part = sem("s_part" + tag)
        block = ctx.enter_context(nc.Block())

        @block.sync
        def _(sp):
            sp.dma_start(k.X[:, :, :], table.rearrange("(t p) d -> p t d", p=B)).then_inc(s_x, 16)
            sp.wait_ge(s_used, NB)
            sp.dma_start(out.rearrange("(t p) d -> p t d", p=B), k.X[:, :, :]).then_inc(s_o, 16)
            sp.wait_ge(s_o, 16)

        @block.gpsimd
        def _(pool):
            for t in range(NB):
                if t >= R:
                    pool.wait_ge(s_used, t - R + 1)
                for n in range(top):
                    pool.indirect_dma_start(
                        out=got[:, t % R, n, :], out_offset=None, in_=k.yg_dram,
                        in_offset=bass.IndirectOffsetOnAxis(ap=k.slot[:, n, t:t + 1], axis=0)).then_inc(s_got[t % R], 16)

        @block.vector
        def _(dve):
            dve.wait_ge(s_x, 16)
            for t in range(NB):
                x = k.X[:, t, :]
                dve.wait_ge(s_got[t % R], (t // R + 1) * 16 * top)
                if relu:
                    dve.scalar_tensor_tensor(x, got[:, t % R, 0, :], 0.0, x, ALU.max, ALU.add).then_inc(s_used, 1)
                else:
                    dve.scalar_tensor_tensor(x, got[:, t % R, 0, :], k.gate[:, 0, t:t + 1], x,
                                             ALU.mult, ALU.add).then_inc(s_part, 1)
                    dve.wait_ge(s_part, t + 1)
                    dve.scalar_tensor_tensor(x, got[:, t % R, 1, :], k.gate[:, 1, t:t + 1], x,
                                             ALU.mult, ALU.add).then_inc(s_used, 1)
                if not relu:
                    dve.wait_ge(s_used, t + 1)
                    dve.bn_stats(k.stat[:, t, :], x)


def batch_norm(nc, k, a):
    with ExitStack() as ctx:
        sb, ps, sem = new(nc, ctx)
        par = sb("bn_par", [128, 3, DIM])
        zero = sb("bn_zero", [B, DIM])
        mean = sb("bn_mean", [128, DIM])
        var, root, gain, tmp = (sb("bn_" + n, [128, DIM]) for n in ("var", "root", "gain", "tmp"))
        sq = sb("bn_sq", [B, 2, DIM])
        yv = sb("bn_y", [B, 2, DIM])
        p_m, p_v = ps("p_bnm"), ps("p_bnv")
        s_par, s_x, s_st, s_z, s_agg, s_sum, s_link, s_root, s_done = (
            sem("s_bn" + n) for n in ("par", "x", "st", "z", "agg", "sum", "link", "root", "done"))
        s_d, s_q, s_u = ([sem(f"s_bn{n}{h}") for h in range(2)] for n in ("d", "q", "u"))
        s_a, s_b = ([sem(f"s_bn{n}{h}") for h in range(2)] for n in ("a", "b"))
        block = ctx.enter_context(nc.Block())

        @block.sync
        def _(sp):
            for n, name in enumerate(("L1_gnn_bias", "L1_gnn_bn_gamma", "L1_gnn_bn_beta")):
                sp.dma_start(par[:, n, :], rep(a[name], 128)).then_inc(s_par, 16)
            sp.dma_start(k.X[:, :, :], k.x2_dram.rearrange("(t p) d -> p t d", p=B)).then_inc(s_x, 16)
            sp.wait_ge(s_done, NB)
            sp.dma_start(k.x3_dram.rearrange("(t p) d -> p t d", p=B), k.X[:, :, :]).then_inc(s_st, 16)
            sp.wait_ge(s_st, 16)

        @block.tensor
        def _(pe):
            pe.wait_ge(s_z, 1)
            pe.matmul(p_m[:, 0:DIM], zero[:, 0:128], zero[:, :], start=True, stop=False, skip_group_check=True)
            with pe.Fori(0, NB) as t:
                pe.wait_ge(s_agg, t + 1)
                pe.matmul(p_m[:, 0:DIM], k.ones[0:B, :], k.acc[:, bass.ds(t, 1), :].rearrange("p o d -> p (o d)"),
                          start=False, stop=False, skip_group_check=True)
            pe.matmul(p_m[:, 0:DIM], zero[:, 0:128], zero[:, :], start=False, stop=True,
                      skip_group_check=True).then_inc(s_sum, 1)
            pe.matmul(p_v[:, 0:DIM], zero[:, 0:128], zero[:, :], start=True, stop=False, skip_group_check=True)
            with pe.Fori(0, NB // 2) as i:
                for h in range(2):
                    pe.wait_ge(s_q[h], i + 1)
                    pe.matmul(p_v[:, 0:DIM], k.ones[0:B, :], sq[:, h, :], start=False, stop=False,
                              skip_group_check=True).then_inc(s_u[h], 1)
            pe.matmul(p_v[:, 0:DIM], zero[:, 0:128], zero[:, :], start=False, stop=True,
                      skip_group_check=True).then_inc(s_sum, 1)

        @block.scalar
        def _(act):
            with act.Fori(0, NB // 2) as i:
                for h in range(2):
                    act.wait_ge(s_d[h], i + 1)
                    act.wait_ge(s_u[h], i)
                    act.activation(sq[:, h, :], k.acc[:, bass.ds(2 * i + h, 1), :].rearrange("p o d -> p (o d)"),
                                   ACT.Square).then_inc(s_q[h], 1)
            act.wait_ge(s_root, 1)
            act.activation(root[:, :], var[:, :], ACT.Sqrt).then_inc(s_root, 1)

        @block.vector
        def _(dve):
            link = linker(dve, s_link)

            def row(t):
                return t[:, :, :].rearrange("p o d -> p (o d)")

            dve.memset(zero[:, :], 0.0).then_inc(s_z, 1)
            dve.wait_ge(s_par, 48)
            with dve.Fori(0, NB) as t:
                o = row(k.acc[:, bass.ds(t, 1), :])
                dve.scalar_tensor_tensor(o, o, k.norm[:, 1, bass.ds(t, 1)], par[0:B, 0, :],
                                         ALU.mult, ALU.add).then_inc(s_agg, 1)
            dve.wait_ge(s_sum, 1)
            link(dve.tensor_scalar(mean[:, :], p_m[:, 0:DIM], 1.0 / NODES, None, ALU.mult))
            with dve.Fori(0, NB // 2) as i:
                for h in range(2):
                    o = row(k.acc[:, bass.ds(2 * i + h, 1), :])
                    dve.tensor_tensor(o, o, mean[0:B, :], ALU.subtract).then_inc(s_d[h], 1)
            dve.wait_ge(s_sum, 2)
            dve.tensor_scalar(var[:, :], p_v[:, 0:DIM], 1.0 / NODES, BN_EPS, ALU.mult, ALU.add).then_inc(s_root, 1)
            dve.wait_ge(s_root, 2)
            rsqrt(link, dve, gain[:, :], var[:, :], root[:, :], tmp[:, :])
            link(dve.tensor_tensor(gain[:, :], gain[:, :], par[:, 1, :], ALU.mult))
            dve.wait_ge(s_x, 16)
            with dve.Fori(0, NB // 2) as i:
                for h in range(2):
                    dve.tensor_tensor(yv[:, h, :], row(k.acc[:, bass.ds(2 * i + h, 1), :]), gain[0:B, :],
                                      ALU.mult).then_inc(s_a[h], 1)
                for h in range(2):
                    dve.wait_ge(s_a[h], i + 1)
                    dve.tensor_tensor(yv[:, h, :], yv[:, h, :], par[0:B, 2, :], ALU.add).then_inc(s_b[h], 1)
                for h in range(2):
                    x = row(k.X[:, bass.ds(2 * i + h, 1), :])
                    dve.wait_ge(s_b[h], i + 1)
                    dve.scalar_tensor_tensor(x, yv[:, h, :], 0.0, x, ALU.max, ALU.add).then_inc(s_done, 1)
                for h in range(2):
                    dve.wait_ge(s_done, 2 * i + h + 1)
                    dve.bn_stats(row(k.stat[:, bass.ds(2 * i + h, 1), :]), row(k.X[:, bass.ds(2 * i + h, 1), :]))


def clear_slots(nc, k):
    with ExitStack() as ctx:
        sb, ps, sem = new(nc, ctx)
        zero = sb("slot_zero", [128, 8, DIM])
        s_z, s_o = sem("s_cz"), sem("s_co")
        block = ctx.enter_context(nc.Block())
        n = (NT0 + 2) // 4

        @block.vector
        def _(dve):
            dve.memset(zero[:, :, :], 0.0).then_inc(s_z, 1)

        @block.sync
        def _(sp):
            sp.wait_ge(s_z, 1)
            for c in range(n):
                sp.dma_start(k.xg_dram.rearrange("(n t p) d -> n p t d", n=n, p=128)[c], zero[:, 0:4, :]).then_inc(s_o, 16)
            sp.wait_ge(s_o, 16 * n)


def turn_router(nc, k, a, wr):
    with ExitStack() as ctx:
        sb, ps, sem = new(nc, ctx)
        p = ps("p_wr")
        s_l, s_T = sem("s_wrl"), sem("s_wrT")
        block = ctx.enter_context(nc.Block())

        @block.sync
        def _(sp):
            sp.dma_start(wr[:, :], a["L1_ffn_router_w"]).then_inc(s_l, 16)

        @block.tensor
        def _(pe):
            pe.wait_ge(s_l, 16)
            for c in range(KC):
                ins = pe.transpose(p[:, c * E1:(c + 1) * E1], wr[:, c * 128:(c + 1) * 128], k.ident[0:E1, 0:E1])
            ins.then_inc(s_T, 1)

        @block.vector
        def _(dve):
            dve.wait_ge(s_T, 1)
            dve.tensor_copy(k.wrT[:, :, :].rearrange("p c e -> p (c e)"), p[:, 0:KC * E1])


def build(nc, a, scratch, upto=99):
    k = Parts()
    k.blk_dram = scratch("blk_dram", (STEPS,), I32)
    k.part_dram = scratch("part_dram", (STEPS, 2 * B), F32)
    k.table1 = scratch("table1", (NODES, HID), F32)
    k.table2 = scratch("table2", (NODES, HID), F32)
    k.table3 = scratch("table3", (NODES, DIM), F32)
    k.x1_dram = scratch("x1", (NODES, DIM), F32)
    k.x2_dram = scratch("x2", (NODES, DIM), F32)
    k.x3_dram = scratch("x3", (NODES, DIM), F32)
    k.xg_dram = scratch("xg", ((NT0 + 2) * TT, DIM), F32)
    k.yg_dram = scratch("yg", (NT0 * TT, DIM), F32)
    with ExitStack() as ctx:
        sb, ps, sem = new(nc, ctx)
        k.iota = sb("iota", [128, 128])
        k.col = sb("col", [128, 1])
        k.ident = sb("ident", [128, 128])
        k.later = sb("later", [128, 128])
        k.ones = sb("ones", [128, 128])
        k.src_idx = sb("src_idx", [ET, SPAD], I32)
        k.dst_rel = sb("dst_rel", [ET, SPAD])
        k.edge_ow = sb("edge_ow", [ET, SPAD, 2])
        k.step_blk = sb("step_blk", [1, STEPS], I32)
        k.norm = sb("norm", [B, 2, NB])
        k.stat = sb("stat", [B, NB, 6])
        k.slot = sb("slot", [B, TOPK, NB], I32)
        k.gate = sb("gate", [B, TOPK, NB])
        k.tile_exp = sb("tile_exp", [1, NT0 + 2], I32)
        clear_slots(nc, k)
        schedule(nc, k, a)
        degrees(nc, k, a)
        with ExitStack() as scope:
            k.acc = new(nc, scope)[0]("acc", [B, NB, HID])
            with ExitStack() as inner:
                k.X = new(nc, inner)[0]("X1", [B, NB, DIM])
                load_rows(nc, k, a["x"], "1")
                project(nc, k, "g1", a["L0_gnn_W1"].rearrange("(c p) n -> p c n", p=128), HID, k.acc, k.norm[:, 0, :])
            store_rows(nc, "t1", k.acc[:, :, :], k.table1)
            aggregate(nc, k, "a1", k.table1, HID, k.acc, False)
            hidden(nc, k, a)
            store_rows(nc, "t2", k.acc[:, :, :], k.table2)
            aggregate(nc, k, "a2", k.table2, HID, k.acc, False)
            k.X = new(nc, scope)[0]("X2", [B, NB, DIM])
            k.logits = new(nc, scope)[0]("logits0", [B, NB, E0])
            conv_out(nc, k, a)
            project(nc, k, "r0", a["L0_ffn_Wr"].rearrange("(c p) n -> p c n", p=128), E0, k.logits, keep=True)
            renormalise(nc, k)
            route(nc, k, a, "q0", E0, TOPK, a["L0_ffn_br"], NT0)
            dispatch(nc, k, "d0", TOPK)
        if upto == 3:
            return
        first_ffn(nc, k, a)
        with ExitStack() as scope:
            k.X = new(nc, scope)[0]("X3", [B, NB, DIM])
            k.acc = new(nc, scope)[0]("acc3", [B, NB, DIM])
            combine(nc, k, "c0", k.x1_dram, TOPK, k.x2_dram)
            project(nc, k, "g3", a["L1_gnn_weight"].rearrange("(c p) n -> p c n", p=128), DIM, k.acc, k.norm[:, 1, :])
            store_rows(nc, "t3", k.acc[:, :, :], k.table3)
            aggregate(nc, k, "a3", k.table3, DIM, k.acc, True)
            batch_norm(nc, k, a)
            k.logits = new(nc, scope)[0]("logits1", [B, NB, E1])
            with ExitStack() as inner:
                wr = new(nc, inner)[0]("wr_rows", [E1, DIM])
                k.wrT = new(nc, inner)[0]("wrT", [128, KC, E1])
                turn_router(nc, k, a, wr)
                project(nc, k, "r1", None, E1, k.logits, keep=True)
            route(nc, k, a, "q1", E1, 1, a["L1_ffn_router_b"], NT1)
            dispatch(nc, k, "d1", 1)
        second_ffn(nc, k, a)
        with ExitStack() as scope:
            k.X = new(nc, scope)[0]("X4", [B, NB, DIM])
            combine(nc, k, "c1", k.x3_dram, 1, a["out"], relu=True)


_INS = ["x", "src", "dst", "edge_weight", "L0_gnn_W1", "L0_gnn_b1", "L0_gnn_W2", "L0_gnn_b2", "L0_ffn_Wr", "L0_ffn_br",
        "L0_ffn_ln_g", "L0_ffn_ln_b", "L0_ffn_W1", "L0_ffn_b1", "L0_ffn_W2", "L0_ffn_b2", "L1_gnn_weight",
        "L1_gnn_bias", "L1_gnn_bn_gamma", "L1_gnn_bn_beta", "L1_ffn_router_w", "L1_ffn_router_b", "L1_ffn_W1",
        "L1_ffn_b1", "L1_ffn_W2", "L1_ffn_b2"]


def kernel(**inputs):
    import numpy as _np
    import concourse.bacc as _bacc
    from concourse.bass_utils import run_bass_kernel_spmd as _run

    nc = _bacc.Bacc("TRN2", target_bir_lowering=False, num_devices=1)
    arrays, a = {}, {}
    for name in _INS:
        arrays[name] = _np.ascontiguousarray(inputs[name])
        a[name] = nc.dram_tensor(name, arrays[name].shape, mybir.dt.from_np(arrays[name].dtype),
                                 kind="ExternalInput").ap()
    a["out"] = nc.dram_tensor("out", (NODES, DIM), F32, kind="ExternalOutput").ap()
    build(nc, a, lambda name, shape, dt: nc.dram_tensor(name, shape, dt).ap())
    return _run(nc, [arrays], core_ids=[0]).results[0]["out"]
```

```python
from contextlib import ExitStack

import concourse.bass as bass
from concourse import mybir

F32 = mybir.dt.float32
I32 = mybir.dt.int32
ALU = mybir.AluOpType
ACT = mybir.ActivationFunctionType
X = mybir.AxisListType.X

NODES, EDGES, DIM, HID = 6250, 100000, 256, 64
E0, H0, TOPK = 8, 1024, 2
E1, H1 = 32, 64
LN_EPS = BN_EPS = 1e-5

NB = 50
B = NODES // NB
ET = 128
TG = 8
TP = -(-EDGES // (ET * TG))
NT = TP * TG
U = 8
STEPS = -(-(-(-EDGES // ET) + NB - 1) // (2 * U)) * 2 * U
SG = 8
SP = STEPS // SG
SPAD = STEPS + U
KC = DIM // 128
TT = 128
R = 3
NT0 = -(-((TOPK * NODES + E0 * (TT - 1)) // TT) // R) * R
NT1 = -(-((NODES + E1 * (TT - 1)) // TT) // R) * R


class Parts:
    pass


def rep(ap, n):
    return ap.partition_broadcast(n)


def new(nc, ctx):
    taken = []

    def give_back():
        if taken:
            nc.clear_and_free_semaphores(taken)
            nc.all_engine_barrier()

    ctx.callback(give_back)

    def sb(name, shape, dt=F32):
        return ctx.enter_context(nc.sbuf_tensor(name, shape, dt))

    def ps(name):
        return ctx.enter_context(nc.psum_tensor(name, [128, 512], F32))

    def sem(name):
        taken.append(nc.alloc_semaphore(name))
        return taken[-1]

    return sb, ps, sem


def turns(eng, n):
    yield 0
    with eng.Fori(1, n) as i:
        yield i


def due(count):
    return not (isinstance(count, int) and count == 0)


def rows_dma(eng, out, in_, sem):
    eng.dma_start(out[0:B // 16 * 16], in_[0:B // 16 * 16]).then_inc(sem, 16)
    eng.dma_start(out[B // 16 * 16:B], in_[B // 16 * 16:B]).then_inc(sem, 16)


def linker(eng, sem):
    count = [0]

    def link(ins):
        count[0] += 1
        ins.then_inc(sem, 1)
        eng.wait_ge(sem, count[0])

    return link


def schedule(nc, k, a):
    with ExitStack() as ctx:
        sb, ps, sem = new(nc, ctx)
        row_i = sb("row_i", [128, 128], I32)
        col_i = sb("col_i", [128, 1], I32)
        step_i = sb("step_i", [SP, SG], I32)
        step = sb("step", [SP, SG])
        dst_t = sb("dst_t", [TP, TG, ET], I32)
        ends = sb("ends", [TP, 2, TG])
        bound = sb("bound", [128, 2, NB])
        meets = sb("meets", [TP, 2, NB, TG])
        counts = sb("counts", [TP, 2, NB])
        below = sb("below", [128, 2, NB])
        ntile = sb("ntile", [128, NB])
        scan = sb("scan", [128, 2, NB])
        shift = sb("shift", [128, NB])
        cmp = sb("cmp", [SP, SG, NB])
        blk = sb("blk", [SP, SG])
        pick = k.in_blk
        pad_i = sb("pad_i", [NT * ET - EDGES >> 5, 2, 32], I32)
        pad_f = sb("pad_f", [NT * ET - EDGES >> 5, 32])
        off = sb("off", [SP, SG])
        tile_f = sb("tile_f", [SP, SG])
        tile_i = sb("tile_i", [SP, SG], I32)
        base = sb("base", [SP, SG])
        blk_f = sb("blk_f", [SP, SG])
        blk_i = sb("blk_i", [SP, SG], I32)
        rows_i = sb("rows_i", [SP, 2, SG, ET], I32)
        rows = sb("rows", [SP, 3, SG, ET])
        p_cnt = ps("p_cnt")
        p_rows = [ps(f"p_rows{n}") for n in range(6)]
        s_iota, s_pad = sem("s_iota"), sem("s_pad")
        s_edges = [sem(f"s_edges{n}") for n in range(3)]
        s_load = sem("s_load")
        s_link = sem("s_link")
        s_counts = sem("s_counts")
        s_below = sem("s_below")
        s_tile = sem("s_tile")
        s_blk = sem("s_blk")
        s_blkst = sem("s_blkst")
        s_blkld = sem("s_blkld")
        s_rows = [sem(f"s_rows{n}") for n in range(3)]
        s_rowf = sem("s_rowf")
        s_rowT = sem("s_rowT")
        s_col = sem("s_col")
        block = ctx.enter_context(nc.Block())

        @block.sync
        def _(sp):
            sp.wait_ge(s_pad, 3)
            for n, (name, pad) in enumerate((("dst", pad_i[:, 1, :]), ("src", pad_i[:, 0, :]), ("edge_weight", pad_f[:, :]))):
                sp.dma_start(k.edges[name][0:EDGES].rearrange("(k n) -> k n", k=16),
                             a[name].rearrange("(k n) -> k n", k=16)).then_inc(s_edges[n], 16)
                sp.dma_start(k.edges[name][EDGES:NT * ET].rearrange("(k n) -> k n", n=32), pad).then_inc(s_edges[n], 16)
            sp.wait_ge(s_edges[0], 32)
            sp.dma_start(dst_t[:, :, :], k.edges["dst"].rearrange("(g p e) -> p g e", p=TP, e=ET)).then_inc(s_load, 16)
            sp.wait_ge(s_blk, 1)
            sp.dma_start(k.blk_dram.rearrange("(g p) -> p g", p=SP), blk_i[:, :],
                         allow_slow_non_contiguous=True).then_inc(s_blkst, 16)
            sp.wait_ge(s_blkst, 16)
            sp.dma_start(k.step_blk[0:1, :], k.blk_dram.rearrange("(o s) -> o s", o=1)).then_inc(s_blkld, 16)
            sp.wait_ge(s_blkld, 16)

        @block.gpsimd
        def _(pool):
            pool.iota(row_i[:, :], pattern=[[1, 128]], base=0, channel_multiplier=0).then_inc(s_iota, 1)
            pool.iota(col_i[:, :], pattern=[[1, 1]], base=0, channel_multiplier=1).then_inc(s_iota, 1)
            pool.iota(step_i[:, :], pattern=[[SP, SG]], base=0, channel_multiplier=1).then_inc(s_iota, 1)
            pool.wait_ge(s_tile, 1)
            for n in range(3):
                pool.wait_ge(s_edges[n], 32)
            for n, name in enumerate(("src", "dst", "edge_weight")):
                table = k.edges[name].rearrange("(t e) -> t e", e=ET)
                for g in range(SG):
                    out = rows_i[:, n, g, :] if n < 2 else rows[:, 2, g, :]
                    pool.indirect_dma_start(
                        out=out, out_offset=None, in_=table,
                        in_offset=bass.IndirectOffsetOnAxis(ap=tile_i[:, g:g + 1], axis=0)).then_inc(s_rows[n], 16)

        @block.vector
        def _(dve):
            link = linker(dve, s_link)
            dve.memset(pad_i[:, 0, :], 0).then_inc(s_pad, 1)
            dve.memset(pad_i[:, 1, :], NODES + B).then_inc(s_pad, 1)
            dve.memset(pad_f[:, :], 0.0).then_inc(s_pad, 1)
            dve.memset(k.ones[:, :], 1.0)
            dve.memset(k.src_idx[:, STEPS:SPAD], 0)
            dve.memset(k.dst_rel[:, STEPS:SPAD], -1.0)
            dve.memset(k.weight[:, STEPS:SPAD], 0.0)
            dve.wait_ge(s_iota, 3)
            dve.tensor_copy(k.iota[:, :], row_i[:, :])
            dve.tensor_copy(step[:, :], step_i[:, :])
            link(dve.tensor_copy(k.col[:, :], col_i[:, :]))
            dve.tensor_scalar(k.ident[:, :], k.iota[:, :], k.col[:, 0:1], None, ALU.is_equal)
            dve.tensor_scalar(k.later[:, :], k.iota[:, :], k.col[:, 0:1], None, ALU.is_gt)
            dve.tensor_scalar(bound[:, 0, :], k.iota[:, 0:NB], float(B), None, ALU.mult)
            dve.tensor_scalar(bound[:, 1, :], k.iota[:, 0:NB], float(B), float(B), ALU.mult, ALU.add)
            dve.wait_ge(s_load, 16)
            dve.tensor_copy(ends[:, 0, :], dst_t[:, :, ET - 1])
            link(dve.tensor_copy(ends[:, 1, :], dst_t[:, :, 0]))
            for n in range(2):
                link(dve.tensor_tensor(meets[:, n, :, :], ends[:, n, :].unsqueeze(1).to_broadcast([TP, NB, TG]),
                                       bound[0:TP, n, :].unsqueeze(2).to_broadcast([TP, NB, TG]), ALU.is_lt))
            dve.tensor_reduce(counts[:, :, :], meets[:, :, :, :], X, ALU.add).then_inc(s_counts, 1)
            dve.wait_ge(s_below, 1)
            link(dve.tensor_copy(below[:, :, :].rearrange("p n b -> p (n b)"), p_cnt[:, 0:2 * NB]))
            link(dve.tensor_tensor(ntile[:, :], below[:, 1, :], below[:, 0, :], ALU.subtract))
            link(dve.tensor_copy(scan[:, 0, :], ntile[:, :]))
            d, at = 1, 0
            while d < NB:
                dve.tensor_copy(scan[:, 1 - at, 0:d], scan[:, at, 0:d])
                link(dve.tensor_tensor(scan[:, 1 - at, d:NB], scan[:, at, d:NB], scan[:, at, 0:NB - d], ALU.add))
                d, at = 2 * d, 1 - at
            ends_at = scan[:, at, :]
            link(dve.tensor_tensor(shift[:, :], below[:, 1, :], ends_at, ALU.subtract))
            link(dve.tensor_tensor(cmp[:, :, :], ends_at[0:SP].unsqueeze(1).to_broadcast([SP, SG, NB]),
                                   step[:, :].unsqueeze(2).to_broadcast([SP, SG, NB]), ALU.is_le))
            link(dve.tensor_reduce(blk[:, :], cmp[:, :, :], X, ALU.add))
            link(dve.tensor_tensor(pick[:, :, :], k.iota[0:SP, 0:NB].unsqueeze(1).to_broadcast([SP, SG, NB]),
                                   blk[:, :].unsqueeze(2).to_broadcast([SP, SG, NB]), ALU.is_equal))
            link(dve.tensor_tensor(cmp[:, :, :], pick[:, :, :],
                                   shift[0:SP, :].unsqueeze(1).to_broadcast([SP, SG, NB]), ALU.mult))
            link(dve.tensor_reduce(off[:, :], cmp[:, :, :], X, ALU.add))
            link(dve.tensor_tensor(tile_f[:, :], step[:, :], off[:, :], ALU.add))
            dve.tensor_scalar(tile_i[:, :], tile_f[:, :], float(NT - 1), 0.0, ALU.min, ALU.max).then_inc(s_tile, 1)
            dve.tensor_scalar(blk_i[:, :], blk[:, :], float(NB - 1), None, ALU.min).then_inc(s_blk, 1)
            link(dve.tensor_scalar(base[:, :], blk[:, :], float(B), None, ALU.mult))
            dve.wait_ge(s_rows[0], 16 * SG)
            dve.tensor_copy(rows[:, 0, :, :], rows_i[:, 0, :, :]).then_inc(s_rowf, 1)
            dve.wait_ge(s_rows[1], 16 * SG)
            link(dve.tensor_copy(rows[:, 1, :, :], rows_i[:, 1, :, :]))
            dve.tensor_tensor(rows[:, 1, :, :], rows[:, 1, :, :],
                              base[:, :].unsqueeze(2).to_broadcast([SP, SG, ET]), ALU.subtract).then_inc(s_rowf, 1)

        @block.tensor
        def _(pe):
            pe.wait_ge(s_counts, 1)
            pe.matmul(p_cnt[:, 0:2 * NB], k.ones[0:TP, :], counts[:, :, :].rearrange("p n b -> p (n b)"),
                      start=True, stop=True).then_inc(s_below, 1)
            for n in range(3):
                if n < 2:
                    pe.wait_ge(s_rowf, n + 1)
                else:
                    pe.wait_ge(s_rows[2], 16 * SG)
                for g in range(SG):
                    last = pe.transpose(p_rows[2 * n + g // 4][0:ET, (g % 4) * SP:(g % 4 + 1) * SP],
                                        rows[:, n, g, :], k.ident[0:SP, 0:SP])
                last.then_inc(s_rowT, 1)

        @block.scalar
        def _(act):
            for n, out in enumerate((k.src_idx, k.dst_rel, k.weight)):
                act.wait_ge(s_rowT, n + 1)
                for half in range(2):
                    act.copy(out[:, half * 4 * SP:(half + 1) * 4 * SP], p_rows[2 * n + half][0:ET, 0:4 * SP])


def rsqrt(link, dve, out, x, root, tmp):
    link(dve.reciprocal(out, root))
    link(dve.tensor_tensor(tmp, out, out, ALU.mult))
    link(dve.tensor_tensor(tmp, tmp, x, ALU.mult))
    link(dve.tensor_scalar(tmp, tmp, -0.5, 1.5, ALU.mult, ALU.add))
    link(dve.tensor_tensor(out, out, tmp, ALU.mult))


def degrees(nc, k, a):
    TURNS = STEPS // (2 * U)
    BF16 = mybir.dt.bfloat16
    with ExitStack() as ctx:
        sb, ps, sem = new(nc, ctx)
        sel = sb("sel_deg", [ET, 2, U, B], BF16)
        parts = sb("w_parts", [ET, SPAD, 4], BF16)
        left = sb("w_left", [ET, SPAD])
        ring = sb("w_ring", [ET, 2, U, 4], BF16)
        sums = sb("step_sums", [B, STEPS, 4])
        both = sb("step_both", [B, 2, STEPS])
        bothT = sb("step_bothT", [SP, 2, SG, B])
        deg, live, root, tmp = (sb(n + "_deg", [B, 2, NB]) for n in ("deg", "live", "root", "tmp"))
        p_sum = [ps(f"p_dsum{h}") for h in range(2)]
        p_T = [ps(f"p_dT{n}") for n in range(4)]
        p_deg = ps("p_deg")
        s_sel, s_ring, s_mm, s_out = ([sem(f"s_d{n}{h}") for h in range(2)] for n in ("sel", "ring", "mm", "out"))
        s_w, s_both, s_T, s_c, s_deg, s_root, s_link = (sem("s_d" + n) for n in ("w", "both", "T", "c", "deg", "root", "link"))
        block = ctx.enter_context(nc.Block())

        @block.vector
        def _(dve):
            link = linker(dve, s_link)
            dve.memset(parts[:, :, 0], 1.0)
            link(dve.tensor_copy(parts[:, :, 1], k.weight[:, :]))
            link(dve.tensor_tensor(left[:, :], k.weight[:, :], parts[:, :, 1], ALU.subtract))
            link(dve.tensor_copy(parts[:, :, 2], left[:, :]))
            link(dve.tensor_tensor(left[:, :], left[:, :], parts[:, :, 2], ALU.subtract))
            dve.tensor_copy(parts[:, :, 3], left[:, :]).then_inc(s_w, 1)
            for i in turns(dve, TURNS):
                for h in range(2):
                    if due(i):
                        dve.wait_ge(s_mm[h], i)
                    dve.tensor_tensor(sel[:, h, :, :], k.iota[:, 0:B].unsqueeze(1).to_broadcast([ET, U, B]),
                                      k.dst_rel[:, bass.ds(i * 2 * U + h * U, U)].unsqueeze(2).to_broadcast([ET, U, B]),
                                      ALU.is_equal).then_inc(s_sel[h], 1)
            dve.wait_ge(k.s_x, 32)
            for t in turns(dve, NB):
                dve.bn_stats(k.stat[:, bass.ds(t, 1), :].rearrange("p o s -> p (o s)"),
                             k.X[:, bass.ds(t, 1), :].rearrange("p o d -> p (o d)"))
            for h in range(2):
                dve.wait_ge(s_out[h], TURNS)
            dve.tensor_copy(both[:, 0, :], sums[:, :, 0])
            dve.tensor_reduce(both[:, 1, :], sums[:, :, 1:4], X, ALU.add).then_inc(s_both, 1)
            dve.wait_ge(s_deg, 1)
            link(dve.tensor_scalar(deg[:, :, :].rearrange("p n b -> p (n b)"), p_deg[0:B, 0:2 * NB], 1.0, None, ALU.add))
            link(dve.tensor_scalar(live[:, :, :], deg[:, :, :], 0.0, None, ALU.is_gt))
            dve.tensor_scalar(deg[:, :, :], deg[:, :, :], 1e-30, None, ALU.max).then_inc(s_root, 1)
            dve.wait_ge(s_root, 2)
            rsqrt(link, dve, k.norm[:, :, :], deg[:, :, :], root[:, :, :], tmp[:, :, :])
            link(dve.tensor_tensor(k.norm[:, :, :], k.norm[:, :, :], live[:, :, :], ALU.mult))

        @block.scalar
        def _(act):
            act.wait_ge(s_w, 1)
            act.copy(ring[:, 0, :, :], parts[:, 0:U, :]).then_inc(s_ring[0], 1)
            for i in turns(act, TURNS):
                for h in range(2):
                    n = i + h
                    if due(n):
                        act.wait_ge(s_mm[1 - h], n)
                    act.copy(ring[:, 1 - h, :, :], parts[:, bass.ds(i * 2 * U + (h + 1) * U, U), :]).then_inc(s_ring[1 - h], 1)
                    act.wait_ge(s_mm[h], i + 1)
                    act.copy(sums[:, bass.ds(i * 2 * U + h * U, U), :].rearrange("p s c -> p (s c)"),
                             p_sum[h][0:B, 0:4 * U]).then_inc(s_out[h], 1)
            for n in range(4):
                act.wait_ge(s_T, n + 1)
                act.copy(bothT[:, n // 2, (n % 2) * 4:(n % 2 + 1) * 4, :].rearrange("p g b -> p (g b)"),
                         p_T[n][0:SP, 0:4 * B]).then_inc(s_c, 1)
            act.wait_ge(s_root, 1)
            act.activation(root[:, :, :], deg[:, :, :], ACT.Sqrt).then_inc(s_root, 1)

        @block.tensor
        def _(pe):
            for i in turns(pe, TURNS):
                for h in range(2):
                    pe.wait_ge(s_sel[h], i + 1)
                    pe.wait_ge(s_ring[h], i + 1)
                    if due(i):
                        pe.wait_ge(s_out[h], i)
                    for u in range(U):
                        ins = pe.matmul(p_sum[h][0:B, 4 * u:4 * u + 4], sel[:, h, u, :], ring[:, h, u, :],
                                        start=True, stop=True)
                    ins.then_inc(s_mm[h], 1)
            pe.wait_ge(s_both, 1)
            for n in range(4):
                for g in range(4):
                    at = ((n % 2) * 4 + g) * SP
                    ins = pe.transpose(p_T[n][0:SP, g * B:(g + 1) * B], both[:, n // 2, at:at + SP], k.ident[0:B, 0:B])
                ins.then_inc(s_T, 1)
            pe.wait_ge(s_c, 4)
            for n in range(2):
                for g in range(SG):
                    ins = pe.matmul(p_deg[0:B, n * NB:(n + 1) * NB], bothT[:, n, g, :], k.in_blk[:, g, :],
                                    start=(g == 0), stop=(g == SG - 1))
            ins.then_inc(s_deg, 1)


def stats_of(link, dve, s_root, stat, eps, mean, rstd, var, root, tmp):
    link(dve.tensor_tensor(mean, stat[:, :, 1], stat[:, :, 4], ALU.add))
    link(dve.tensor_tensor(tmp, stat[:, :, 1], stat[:, :, 4], ALU.subtract))
    link(dve.tensor_tensor(tmp, tmp, tmp, ALU.mult))
    link(dve.tensor_tensor(var, stat[:, :, 2], stat[:, :, 5], ALU.add))
    link(dve.tensor_scalar(mean, mean, 0.5, None, ALU.mult))
    link(dve.tensor_scalar(var, var, 1.0 / DIM, eps, ALU.mult, ALU.add))
    link(dve.scalar_tensor_tensor(var, tmp, 0.25, var, ALU.mult, ALU.add))
    ins = dve.tensor_scalar(var, var, 0.0, None, ALU.max)
    ins.then_inc(s_root, 1)
    dve.wait_ge(s_root, 2)
    rsqrt(link, dve, rstd, var, root, tmp)


def issue_rows(eng, k, table, sem):
    rows_dma(eng, k.X, table.rearrange("(t p) d -> p t d", p=B), sem)


def project(nc, k, tag, weight, M, out, scale=None, keep=False):
    with ExitStack() as ctx:
        sb, ps, sem = new(nc, ctx)
        w = k.wrT if weight is None else sb("w_" + tag, [128, KC, M])
        mean, rstd, var, root, tmp = (sb(n + tag, [B, NB]) for n in ("mean", "rstd", "var", "root", "tmp"))
        z = sb("z_" + tag, [B, 2, DIM])
        zT = sb("zT_" + tag, [128, 2, KC, B])
        p_zT = [ps(f"p_zT{h}_{tag}") for h in range(2)]
        p_y = [ps(f"p_y{h}_{tag}") for h in range(2)]
        s_w, s_link, s_root = sem("s_w" + tag), sem("s_l" + tag), sem("s_r" + tag)
        s_z, s_T, s_c, s_mm, s_y = ([sem(f"s_{n}{h}_{tag}") for h in range(2)] for n in ("z", "T", "c", "mm", "y"))
        block = ctx.enter_context(nc.Block())

        if weight is not None:
            @block.sync
            def _(sp):
                sp.dma_start(w[:, :, :], weight).then_inc(s_w, 16)

        @block.vector
        def _(dve):
            link = linker(dve, s_link)
            stats_of(link, dve, s_root, k.stat, LN_EPS, mean[:, :], rstd[:, :], var[:, :], root[:, :], tmp[:, :])
            for i in turns(dve, NB // 2):
                for h in range(2):
                    x = k.X[:, bass.ds(2 * i + h, 1), :].rearrange("p o d -> p (o d)")
                    m, r = mean[:, bass.ds(2 * i + h, 1)], rstd[:, bass.ds(2 * i + h, 1)]
                    if due(i):
                        dve.wait_ge(s_T[h], i)
                    dve.tensor_scalar(z[:, h, :], x, m, r, ALU.subtract, ALU.mult).then_inc(s_z[h], 1)
                    if keep:
                        dve.tensor_scalar(x, x, m, r, ALU.subtract, ALU.mult)

        @block.tensor
        def _(pe):
            if weight is not None:
                pe.wait_ge(s_w, 16)
            for i in turns(pe, NB // 2):
                for h in range(2):
                    pe.wait_ge(s_z[h], i + 1)
                    if due(i):
                        pe.wait_ge(s_c[h], i)
                    for c in range(KC):
                        ins = pe.transpose(p_zT[h][:, c * B:(c + 1) * B], z[:, h, c * 128:(c + 1) * 128],
                                           k.ident[0:B, 0:B])
                    ins.then_inc(s_T[h], 1)
                for h in range(2):
                    pe.wait_ge(s_c[h], i + 1)
                    if due(i):
                        pe.wait_ge(s_y[h], i)
                    for c in range(KC):
                        ins = pe.matmul(p_y[h][0:B, 0:M], zT[:, h, c, :], w[:, c, :], start=(c == 0), stop=(c == KC - 1))
                    ins.then_inc(s_mm[h], 1)

        @block.scalar
        def _(act):
            act.wait_ge(s_root, 1)
            act.activation(root[:, :], var[:, :], ACT.Sqrt).then_inc(s_root, 1)
            for i in turns(act, NB // 2):
                for h in range(2):
                    act.wait_ge(s_T[h], i + 1)
                    if due(i):
                        act.wait_ge(s_mm[h], i)
                    act.copy(zT[:, h, :, :].rearrange("p c b -> p (c b)"), p_zT[h][:, 0:KC * B]).then_inc(s_c[h], 1)
                for h in range(2):
                    act.wait_ge(s_mm[h], i + 1)
                    o = out[:, bass.ds(2 * i + h, 1), :].rearrange("p o m -> p (o m)")
                    if scale is None:
                        act.copy(o, p_y[h][0:B, 0:M]).then_inc(s_y[h], 1)
                    else:
                        act.activation(o, p_y[h][0:B, 0:M], ACT.Copy,
                                       scale=scale[:, bass.ds(2 * i + h, 1)]).then_inc(s_y[h], 1)


def aggregate(nc, k, tag, table, D, acc, weighted):
    TURNS = STEPS // (2 * U)
    with ExitStack() as ctx:
        sb, ps, sem = new(nc, ctx)
        rows = sb("rows_" + tag, [ET, 2, U, D])
        idx = sb("idx_" + tag, [ET, 2, U], I32)
        sel = sb("sel_" + tag, [ET, 2, U, B])
        turn = sb("turn_" + tag, [1, 3])
        credit = sb("credit_" + tag, [1, 1])
        p_sum = [ps(f"p_sum{u}_{tag}") for u in range(U)]
        s_one, s_turn = sem("s_one" + tag), sem("s_turn" + tag)
        s_idx, s_rows, s_sel, s_sum, s_done = ([sem(f"s_{n}{h}_{tag}") for h in range(2)]
                                               for n in ("idx", "rows", "sel", "sum", "done"))
        block = ctx.enter_context(nc.Block())

        @block.scalar
        def _(act):
            for i in turns(act, TURNS):
                for h in range(2):
                    if due(i * U * 16):
                        act.wait_ge(s_rows[h], i * U * 16)
                    act.copy(idx[:, h, :], k.src_idx[:, bass.ds(i * 2 * U + h * U, U)]).then_inc(s_idx[h], 1)

        @block.gpsimd
        def _(pool):
            pool.memset(turn[:, :], 0.0).then_inc(s_one, 1)
            pool.wait_ge(s_one, 1)
            for i in turns(pool, TURNS):
                for h in range(2):
                    if due(2 * i + h):
                        pool.wait_ge(s_turn, 2 * i + h)
                    pool.wait_ge(s_idx[h], i + 1)
                    if due(i * U):
                        pool.wait_ge(s_sum[h], i * U)
                    pool.tensor_tensor(turn[:, 2:3], turn[:, 0:1], turn[:, 1:2], ALU.add).then_inc(s_turn, 1)
                    for u in range(U):
                        pool.indirect_dma_start(
                            out=rows[:, h, u, :], out_offset=None, in_=table,
                            in_offset=bass.IndirectOffsetOnAxis(ap=idx[:, h, u:u + 1], axis=0)).then_inc(s_rows[h], 16)

        @block.vector
        def _(dve):
            def select(h, at, used):
                if due(used):
                    dve.wait_ge(s_sum[h], used * U)
                if weighted:
                    for u in range(U):
                        dve.tensor_scalar(sel[:, h, u, :], k.iota[:, 0:B], k.dst_rel[:, bass.ds(at + u, 1)],
                                          k.weight[:, bass.ds(at + u, 1)], ALU.is_equal, ALU.mult).then_inc(s_sel[h], 1)
                else:
                    dve.tensor_tensor(sel[:, h, :, :], k.iota[:, 0:B].unsqueeze(1).to_broadcast([ET, U, B]),
                                      k.dst_rel[:, bass.ds(at, U)].unsqueeze(2).to_broadcast([ET, U, B]),
                                      ALU.is_equal).then_inc(s_sel[h], U)

            dve.memset(credit[:, :], 0.0).then_inc(s_done[1], U)
            select(0, 0, 0)
            for i in turns(dve, TURNS):
                for h in range(2):
                    select(1 - h, i * 2 * U + (h + 1) * U, i + h)
                    _, b = nc.values_load_multi_w_load_instructions(
                        k.step_blk[0:1, bass.ds(i * 2 * U + h * U, U)], engines=[mybir.EngineType.DVE],
                        min_val=0, max_val=NB - 1, skip_runtime_bounds_check_because="the schedule clamps it")
                    for u in range(U):
                        dve.wait_ge(s_sum[h], i * U + u + 1)
                        dve.wait_ge(s_done[h] if u else s_done[1 - h],
                                    i * U + u + h * U if u else i * U + U)
                        o = acc[:, bass.ds(b[u], 1), :].rearrange("p o d -> p (o d)")
                        dve.tensor_tensor(o, o, p_sum[u][0:B, 0:D], ALU.add).then_inc(s_done[h], 1)

        @block.tensor
        def _(pe):
            for i in turns(pe, TURNS):
                for h in range(2):
                    pe.wait_ge(s_rows[h], (i + 1) * U * 16)
                    for u in range(U):
                        pe.wait_ge(s_sel[h], i * U + u + 1)
                        pe.wait_ge(s_done[1 - h], i * U + u + 1)
                        pe.matmul(p_sum[u][0:B, 0:D], sel[:, h, u, :], rows[:, h, u, :],
                                  start=True, stop=True).then_inc(s_sum[h], 1)


def store_rows(nc, tag, src, table):
    with ExitStack() as ctx:
        s = new(nc, ctx)[2]("s_st" + tag)
        block = ctx.enter_context(nc.Block())

        @block.sync
        def _(sp):
            rows_dma(sp, table.rearrange("(t p) d -> p t d", p=B), src, s)
            sp.wait_ge(s, 32)


def hidden(nc, k, a):
    with ExitStack() as ctx:
        sb, ps, sem = new(nc, ctx)
        b1 = sb("b1", [B, HID])
        s_b, s_link = sem("s_b1"), sem("s_hlink")
        block = ctx.enter_context(nc.Block())

        @block.sync
        def _(sp):
            sp.dma_start(b1[:, :], rep(a["L0_gnn_b1"], B)).then_inc(s_b, 16)

        @block.vector
        def _(dve):
            link = linker(dve, s_link)
            norm = k.norm[:, 0, :].unsqueeze(2).to_broadcast([B, NB, HID])
            acc = k.acc[:, :, :]
            link(dve.tensor_tensor(acc, acc, norm, ALU.mult))
            dve.wait_ge(s_b, 16)
            link(dve.tensor_tensor(acc, acc, b1[:, :].unsqueeze(1).to_broadcast([B, NB, HID]), ALU.add))
            link(dve.scalar_tensor_tensor(acc, acc, 0.0, norm, ALU.max, ALU.mult))


def conv_out(nc, k, a):
    with ExitStack() as ctx:
        sb, ps, sem = new(nc, ctx)
        w2 = sb("w2", [128, DIM])
        row = sb("row_w2", [B, 2, 128])
        rowT = sb("rowT_w2", [128, 2, B])
        p_T = [ps(f"p_T{h}_w2") for h in range(2)]
        p_y = [ps(f"p_y{h}_w2") for h in range(2)]
        s_w, s_x, s_one, s_st = sem("s_w_w2"), sem("s_x_w2"), sem("s_one_w2"), sem("s_st_w2")
        s_r, s_T, s_c, s_mm, s_y, s_bn = ([sem(f"s_{n}{h}_w2") for h in range(2)]
                                          for n in ("r", "T", "c", "mm", "y", "bn"))
        block = ctx.enter_context(nc.Block())

        @block.sync
        def _(sp):
            sp.wait_ge(s_one, 1)
            sp.dma_start(w2[0:HID, :], a["L0_gnn_W2"]).then_inc(s_w, 16)
            sp.dma_start(w2[HID:HID + 1, :], a["L0_gnn_b2"].rearrange("(o d) -> o d", o=1)).then_inc(s_w, 16)
            issue_rows(sp, k, a["x"], s_x)
            for h in range(2):
                sp.wait_ge(s_y[h], NB // 2)
            rows_dma(sp, k.x1_dram.rearrange("(t p) d -> p t d", p=B), k.X, s_st)
            sp.wait_ge(s_st, 32)

        @block.scalar
        def _(act):
            for i in turns(act, NB // 2):
                for h in range(2):
                    if due(i):
                        act.wait_ge(s_T[h], i)
                    act.activation(row[:, h, 0:HID], k.acc[:, bass.ds(2 * i + h, 1), :].rearrange("p o d -> p (o d)"),
                                   ACT.Copy, scale=k.norm[:, 0, bass.ds(2 * i + h, 1)]).then_inc(s_r[h], 1)
                for h in range(2):
                    act.wait_ge(s_T[h], i + 1)
                    if due(i):
                        act.wait_ge(s_mm[h], i)
                    act.copy(rowT[:, h, :], p_T[h][:, 0:B]).then_inc(s_c[h], 1)

        @block.tensor
        def _(pe):
            pe.wait_ge(s_w, 32)
            pe.wait_ge(s_one, 3)
            for i in turns(pe, NB // 2):
                for h in range(2):
                    pe.wait_ge(s_r[h], i + 1)
                    if due(i):
                        pe.wait_ge(s_c[h], i)
                    pe.transpose(p_T[h][:, 0:B], row[:, h, :], k.ident[0:B, 0:B]).then_inc(s_T[h], 1)
                for h in range(2):
                    pe.wait_ge(s_c[h], i + 1)
                    if due(i):
                        pe.wait_ge(s_y[h], i)
                    pe.matmul(p_y[h][0:B, 0:DIM], rowT[:, h, :], w2[:, :], start=True, stop=True).then_inc(s_mm[h], 1)

        @block.vector
        def _(dve):
            dve.memset(w2[:, :], 0.0).then_inc(s_one, 1)
            dve.memset(row[:, :, HID:HID + 1], 1.0).then_inc(s_one, 1)
            dve.memset(row[:, :, HID + 1:128], 0.0).then_inc(s_one, 1)
            dve.wait_ge(s_x, 32)
            for i in turns(dve, NB // 2):
                for h in range(2):
                    dve.wait_ge(s_mm[h], i + 1)
                    x = k.X[:, bass.ds(2 * i + h, 1), :].rearrange("p o d -> p (o d)")
                    dve.tensor_tensor(x, x, p_y[h][0:B, 0:DIM], ALU.add).then_inc(s_y[h], 1)
                for h in range(2):
                    dve.wait_ge(s_y[h], i + 1)
                    dve.bn_stats(k.stat[:, bass.ds(2 * i + h, 1), :].rearrange("p o s -> p (o s)"),
                                 k.X[:, bass.ds(2 * i + h, 1), :].rearrange("p o d -> p (o d)"))


def renormalise(nc, k):
    with ExitStack() as ctx:
        sb, ps, sem = new(nc, ctx)
        mean, rstd, var, root, tmp = (sb(n + "rn", [B, NB]) for n in ("mean", "rstd", "var", "root", "tmp"))
        s_link, s_root, s_stat = sem("s_lrn"), sem("s_rrn"), sem("s_srn")
        block = ctx.enter_context(nc.Block())

        @block.vector
        def _(dve):
            link = linker(dve, s_link)
            for t in turns(dve, NB):
                dve.bn_stats(k.stat[:, bass.ds(t, 1), :].rearrange("p o s -> p (o s)"),
                             k.X[:, bass.ds(t, 1), :].rearrange("p o d -> p (o d)")).then_inc(s_stat, 1)
            dve.wait_ge(s_stat, NB)
            stats_of(link, dve, s_root, k.stat, LN_EPS, mean[:, :], rstd[:, :], var[:, :], root[:, :], tmp[:, :])
            for t in turns(dve, NB):
                x = k.X[:, bass.ds(t, 1), :].rearrange("p o d -> p (o d)")
                dve.tensor_scalar(x, x, mean[:, bass.ds(t, 1)], rstd[:, bass.ds(t, 1)], ALU.subtract, ALU.mult)

        @block.scalar
        def _(act):
            act.wait_ge(s_root, 1)
            act.activation(root[:, :], var[:, :], ACT.Sqrt).then_inc(s_root, 1)


def route(nc, k, a, tag, E, top, bias, tiles):
    BE = NB * E
    G = -(-BE // 512)
    while BE % G:
        G += 1
    W = BE // G
    with ExitStack() as ctx:
        sb, ps, sem = new(nc, ctx)
        br = sb("br" + tag, [B, E])
        lg = sb("lg" + tag, [B, NB, E])
        cand = sb("cand" + tag, [B, NB, E])
        hot = sb("hot" + tag, [B, top, NB, E])
        mask = sb("mask" + tag, [B, NB, E])
        scan = sb("scan" + tag, [B, 2, NB, E])
        small = sb("small" + tag, [B, 4, NB])
        cnt = sb("cnt" + tag, [B, E])
        cnt_i = sb("cnt_i" + tag, [B, E], I32)
        til = sb("til" + tag, [B, E])
        tsc = sb("tsc" + tag, [B, 2, E])
        tcmp = sb("tcmp" + tag, [1, tiles + 2, E])
        tf = sb("tf" + tag, [1, tiles + 2])
        tio = sb("tio" + tag, [1, tiles + 2], I32)
        tiof = sb("tiof" + tag, [1, tiles + 2])
        p_rank = [ps(f"p_rank{g}_{tag}") for g in range(G)]
        p_tot = [ps(f"p_tot{g}_{tag}") for g in range(G)]
        s_b, s_link, s_e, s_m, s_p, s_io = (sem(f"s_{n}_{tag}") for n in ("b", "link", "e", "m", "p", "io"))
        block = ctx.enter_context(nc.Block())

        @block.sync
        def _(sp):
            sp.dma_start(br[:, :], rep(bias, B)).then_inc(s_b, 16)

        @block.gpsimd
        def _(pool):
            pool.iota(tio[:, :], pattern=[[1, tiles + 2]], base=0, channel_multiplier=0).then_inc(s_io, 1)

        @block.scalar
        def _(act):
            if top > 1:
                act.wait_ge(s_e, 1)
                act.activation(lg[:, :, :], lg[:, :, :], ACT.Exp).then_inc(s_e, 1)

        @block.tensor
        def _(pe):
            pe.wait_ge(s_m, 1)
            flat = mask[:, :, :].rearrange("p b e -> p (b e)")
            for g in range(G):
                pe.matmul(p_rank[g][0:B, 0:W], k.later[0:B, 0:B], flat[:, g * W:(g + 1) * W], start=True, stop=True)
                ins = pe.matmul(p_tot[g][0:B, 0:W], k.ones[0:B, 0:B], flat[:, g * W:(g + 1) * W], start=True, stop=True)
            ins.then_inc(s_p, 1)

        @block.vector
        def _(dve):
            link = linker(dve, s_link)
            wide = [B, NB, E]

            def per_node(n):
                return small[:, n, :].unsqueeze(2).to_broadcast(wide)

            def per_expert(x):
                return x.unsqueeze(1).to_broadcast(wide)

            dve.wait_ge(s_b, 16)
            link(dve.tensor_tensor(lg[:, :, :], k.logits[:, :, 0:E], per_expert(br[:, :]), ALU.add))
            if top > 1:
                link(dve.tensor_reduce(small[:, 0, :], lg[:, :, :], X, ALU.max))
                dve.tensor_tensor(lg[:, :, :], lg[:, :, :], per_node(0), ALU.subtract).then_inc(s_e, 1)
                dve.wait_ge(s_e, 2)
                link(dve.tensor_reduce(small[:, 0, :], lg[:, :, :], X, ALU.add))
                link(dve.reciprocal(small[:, 0, :], small[:, 0, :]))
                link(dve.tensor_tensor(lg[:, :, :], lg[:, :, :], per_node(0), ALU.mult))
            for n in range(top):
                link(dve.tensor_reduce(small[:, n, :], lg[:, :, :], X, ALU.max))
                link(dve.tensor_tensor(cand[:, :, :], lg[:, :, :], per_node(n), ALU.is_equal))
                link(dve.scalar_tensor_tensor(cand[:, :, :], cand[:, :, :], -64.0, per_expert(k.iota[0:B, 0:E]),
                                              ALU.mult, ALU.add))
                link(dve.tensor_reduce(small[:, 3, :], cand[:, :, :], X, ALU.min))
                link(dve.tensor_tensor(hot[:, n, :, :], cand[:, :, :], per_node(3), ALU.is_equal))
                if n + 1 < top:
                    link(dve.scalar_tensor_tensor(lg[:, :, :], hot[:, n, :, :], -2.0, lg[:, :, :], ALU.mult, ALU.add))
            if top > 1:
                link(dve.tensor_tensor(mask[:, :, :], hot[:, 0, :, :], hot[:, 1, :, :], ALU.add))
                link(dve.tensor_tensor(small[:, 2, :], small[:, 0, :], small[:, 1, :], ALU.add))
            else:
                link(dve.tensor_copy(mask[:, :, :], hot[:, 0, :, :]))
            dve.memset(tf[:, :], 0.0).then_inc(s_m, 1)
            if top > 1:
                link(dve.reciprocal(small[:, 2, :], small[:, 2, :]))
                for n in range(top):
                    dve.tensor_tensor(k.gate[:, n, :], small[:, n, :], small[:, 2, :], ALU.mult)
            dve.wait_ge(s_p, 1)
            for g in range(G):
                dve.tensor_copy(cand[:, :, :].rearrange("p b e -> p (b e)")[:, g * W:(g + 1) * W], p_rank[g][0:B, 0:W])
                link(dve.tensor_copy(scan[:, 0, :, :].rearrange("p b e -> p (b e)")[:, g * W:(g + 1) * W],
                                     p_tot[g][0:B, 0:W]))
            link(dve.tensor_tensor(cand[:, :, :], cand[:, :, :], scan[:, 0, :, :], ALU.subtract))
            d, at = 1, 0
            while d < NB:
                dve.tensor_copy(scan[:, 1 - at, 0:d, :], scan[:, at, 0:d, :])
                link(dve.tensor_tensor(scan[:, 1 - at, d:NB, :], scan[:, at, d:NB, :], scan[:, at, 0:NB - d, :], ALU.add))
                d, at = 2 * d, 1 - at
            link(dve.tensor_tensor(cand[:, :, :], cand[:, :, :], scan[:, at, :, :], ALU.add))
            link(dve.tensor_scalar(cnt[:, :], scan[:, at, NB - 1, :], float(TT - 1), None, ALU.add))
            link(dve.tensor_copy(cnt_i[:, :], cnt[:, :]))
            link(dve.tensor_scalar(cnt_i[:, :], cnt_i[:, :], TT.bit_length() - 1, None, ALU.logical_shift_right))
            link(dve.tensor_copy(til[:, :], cnt_i[:, :]))
            link(dve.tensor_copy(tsc[:, 0, :], til[:, :]))
            d, at = 1, 0
            while d < E:
                dve.tensor_copy(tsc[:, 1 - at, 0:d], tsc[:, at, 0:d])
                link(dve.tensor_tensor(tsc[:, 1 - at, d:E], tsc[:, at, d:E], tsc[:, at, 0:E - d], ALU.add))
                d, at = 2 * d, 1 - at
            ends = tsc[:, at, :]
            dve.wait_ge(s_io, 1)
            link(dve.tensor_copy(tiof[:, :], tio[:, :]))
            link(dve.tensor_tensor(tcmp[:, :, :], ends[0:1].unsqueeze(1).to_broadcast([1, tiles + 2, E]),
                                   tiof[:, :].unsqueeze(2).to_broadcast([1, tiles + 2, E]), ALU.is_le))
            link(dve.tensor_reduce(tf[:, :], tcmp[:, :, :], X, ALU.add))
            dve.tensor_scalar(k.tile_exp[0:1, 0:tiles + 2], tf[:, :], float(E - 1), None, ALU.min)
            link(dve.tensor_tensor(til[:, :], ends, til[:, :], ALU.subtract))
            link(dve.tensor_scalar(til[:, :], til[:, :], float(TT), None, ALU.mult))
            link(dve.tensor_tensor(cand[:, :, :], cand[:, :, :], per_expert(til[:, :]), ALU.add))
            for n in range(top):
                link(dve.tensor_tensor(hot[:, n, :, :], hot[:, n, :, :], cand[:, :, :], ALU.mult))
                link(dve.tensor_reduce(small[:, 3, :], hot[:, n, :, :], X, ALU.add))
                link(dve.tensor_copy(k.slot[:, n, :], small[:, 3, :]))


def dispatch(nc, k, tag, top):
    with ExitStack() as ctx:
        s = new(nc, ctx)[2]("s_disp" + tag)
        block = ctx.enter_context(nc.Block())

        @block.gpsimd
        def _(pool):
            pool.wait_ge(k.s_clear, k.clears)
            for t in range(NB):
                for n in range(top):
                    pool.indirect_dma_start(
                        out=k.xg_dram, out_offset=bass.IndirectOffsetOnAxis(ap=k.slot[:, n, t:t + 1], axis=0),
                        in_=k.X[:, t, :], in_offset=None).then_inc(s, 16)
            pool.wait_ge(s, NB * top * 16)


def expert_bias(nc, k, a, w1, b1T):
    with ExitStack() as ctx:
        sb, ps, sem = new(nc, ctx)
        R = E0 * KC
        HC = H0 // 128
        rows = sb("gb_rows", [R, 2, 128])
        b1r = sb("b1_rows", [E0 * HC, 128])
        gb = sb("gb", [128, 2, R])
        b1c = sb("b1c", [128, E0 * HC])
        p_gb, p_b1, p_sh = ps("p_gb"), ps("p_b1"), ps("p_sh")
        s_ld, s_T, s_c, s_mm = sem("s_ebld"), sem("s_ebT"), sem("s_ebc"), sem("s_ebmm")
        s_w = [sem(f"s_ebw{c}") for c in range(KC)]
        block = ctx.enter_context(nc.Block())

        @block.sync
        def _(sp):
            sp.dma_start(rows[:, 0, :], a["L0_ffn_ln_g"].rearrange("e (c p) -> (e c) p", p=128)).then_inc(s_ld, 16)
            sp.dma_start(rows[:, 1, :], a["L0_ffn_ln_b"].rearrange("e (c p) -> (e c) p", p=128)).then_inc(s_ld, 16)
            sp.dma_start(b1r[:, :], a["L0_ffn_b1"].rearrange("e (c p) -> (e c) p", p=128)).then_inc(s_ld, 16)
            for c in range(KC):
                sp.dma_start(w1[:, c, :].rearrange("p (e h) -> p e h", e=E0),
                             a["L0_ffn_W1"].rearrange("e (c p) h -> c p e h", p=128)[c]).then_inc(s_w[c], 16)

        @block.tensor
        def _(pe):
            pe.wait_ge(s_ld, 48)
            for n in range(2):
                pe.transpose(p_gb[:, n * R:(n + 1) * R], rows[:, n, :], k.ident[0:R, 0:R])
            pe.transpose(p_b1[:, 0:E0 * HC], b1r[:, :], k.ident[0:E0 * HC, 0:E0 * HC]).then_inc(s_T, 1)
            pe.wait_ge(s_c, 1)
            for c in range(KC):
                pe.wait_ge(s_w[c], 16)
            for e in range(E0):
                for m in range(HC):
                    for c in range(KC):
                        ins = pe.matmul(p_sh[:, e * HC + m:e * HC + m + 1], w1[:, c, e * H0 + m * 128:e * H0 + (m + 1) * 128],
                                        gb[:, 1, e * KC + c:e * KC + c + 1], start=(c == 0), stop=(c == KC - 1))
                ins.then_inc(s_mm, 1)

        @block.vector
        def _(dve):
            dve.wait_ge(s_T, 1)
            dve.tensor_copy(b1c[:, :], p_b1[:, 0:E0 * HC])
            dve.tensor_copy(gb[:, :, :].rearrange("p n r -> p (n r)"), p_gb[:, 0:2 * R]).then_inc(s_c, 1)
            dve.wait_ge(s_c, 1)
            for e in range(E0):
                dve.wait_ge(s_mm, e + 1)
                for c in range(KC):
                    w = w1[:, c, e * H0:(e + 1) * H0]
                    dve.tensor_scalar(w, w, gb[:, 0, e * KC + c:e * KC + c + 1], None, ALU.mult)
            dve.tensor_tensor(b1T, b1c[:, :], p_sh[:, 0:E0 * HC], ALU.add)


def experts(nc, k, tag, tiles, E, H, w1, w2, b1T, b2, func):
    HC = -(-H // 128)
    HP = H // HC
    NW = min(H, 512)
    HB = H // NW
    HW = max(H, 128)
    with ExitStack() as ctx:
        sb, ps, sem = new(nc, ctx)
        x = sb("x" + tag, [TT, R, DIM])
        xT = sb("xT" + tag, [128, R, KC, TT])
        hid = sb("hid" + tag, [TT, 1, HW])
        hT = sb("hT" + tag, [HP, 1, HC, TT])
        y = sb("y" + tag, [TT, R, DIM])
        p_x = [ps(f"p_x{n}" + tag) for n in range(1)]
        p_h = [ps(f"p_h{n}_{tag}") for n in range(HB)]
        p_t = [ps(f"p_t{n}_{tag}") for n in range(-(-HC // 4))]
        p_y = ps("p_y" + tag)
        s_x, s_xT, s_xc, s_h, s_hc, s_hT, s_g, s_mm, s_y, s_st = (
            [sem(f"s_{n}{r}_{tag}") for r in range(R)]
            for n in ("x", "xT", "xc", "h", "hc", "hT", "g", "mm", "y", "st"))
        s_wide = sem("s_wide" + tag)
        block = ctx.enter_context(nc.Block())
        src = k.xg_dram.rearrange("(n p) d -> n p d", p=TT)
        dst = k.yg_dram.rearrange("(n p) d -> n p d", p=TT)
        PE, DVE, ACTE = mybir.EngineType.PE, mybir.EngineType.DVE, mybir.EngineType.Activation

        def ahead(r, i, n):
            return (r + n) % R, i + (r + n) // R

        def before(eng, sems, r, i):
            if due(i + (r > 0)):
                eng.wait_ge(sems[(r - 1) % R], i + (1 if r else 0))

        def expert_of(engine, at, n):
            return nc.values_load_multi_w_load_instructions(
                k.tile_exp[0:1, bass.ds(at, n)], engines=[engine], min_val=0, max_val=E - 1,
                skip_runtime_bounds_check_because="route clamps it")[1]

        @block.sync
        def _(sp):
            for i in turns(sp, tiles // R):
                for r in range(R):
                    if due(i):
                        sp.wait_ge(s_xT[r], i)
                    sp.dma_start(x[:, r, :], src[bass.ds(i * R + r, 1)].rearrange("o p d -> (o p) d")).then_inc(s_x[r], 16)
            for r in range(2):
                sp.wait_ge(s_xT[r], tiles // R)
                sp.dma_start(x[:, r, :], src[tiles + r]).then_inc(s_x[r], 16)

        @block.gpsimd
        def _(pool):
            for i in turns(pool, tiles // R):
                for r in range(R):
                    pool.wait_ge(s_y[r], i + 1)
                    pool.dma_start(dst[bass.ds(i * R + r, 1)].rearrange("o p d -> (o p) d"), y[:, r, :]).then_inc(s_st[r], 16)
            for r in range(R):
                pool.wait_ge(s_st[r], tiles // R * 16)

        @block.tensor
        def _(pe):
            def turn_x(r, i):
                pe.wait_ge(s_x[r], i * 16 + 16)
                before(pe, s_xc, r, i)
                for c in range(KC):
                    ins = pe.transpose(p_x[0][:, c * TT:(c + 1) * TT], x[:, r, c * 128:(c + 1) * 128], k.ident[:, :])
                ins.then_inc(s_xT[r], 1)

            def up(r, i, e):
                pe.wait_ge(s_xc[r], i + 1)
                before(pe, s_hc, r, i)
                for n in range(HB):
                    for c in range(KC):
                        ins = pe.matmul(p_h[n][:, 0:NW], xT[:, r, c, :],
                                        w1[:, c, bass.ds(e * H + n * NW, NW)], start=(c == 0), stop=(c == KC - 1))
                ins.then_inc(s_h[r], 1)

            def turn_h(r, i, hh):
                pe.wait_ge(s_hc[r], i + 1)
                before(pe, s_g, r, i)
                for m in range(HC):
                    ins = pe.transpose(p_t[m // 4][:, (m % 4) * TT:(m % 4 + 1) * TT], hid[:, hh, m * 128:(m + 1) * 128],
                                       k.ident[:, :])
                ins.then_inc(s_hT[r], 1)

            def down(r, i, e, hh):
                pe.wait_ge(s_g[r], i + 1)
                before(pe, s_y, r, i)
                for m in range(HC):
                    ins = pe.matmul(p_y[:, 0:DIM], hT[:, hh, m, :], w2[:, m, bass.ds(e * DIM, DIM)],
                                    start=(m == 0), stop=(m == HC - 1))
                ins.then_inc(s_mm[r], 1)

            if HP < 128:
                pe.wait_ge(s_wide, 1)
            turn_x(0, 0)
            (e,) = expert_of(PE, 0, 1)
            up(0, 0, e)
            turn_x(1, 0)
            for i in turns(pe, tiles // R):
                e = expert_of(PE, R * i, R + 1)
                for r in range(R):
                    turn_h(r, i, 0)
                    up(*ahead(r, i, 1), e[r + 1])
                    turn_x(*ahead(r, i, 2))
                    down(r, i, e[r], 0)

        @block.scalar
        def _(act):
            def copy_x(r, i):
                act.wait_ge(s_xT[r], i + 1)
                if due(i):
                    act.wait_ge(s_h[r], i)
                act.copy(xT[:, r, :, :].rearrange("p c t -> p (c t)"), p_x[0][:, 0:KC * TT]).then_inc(s_xc[r], 1)

            copy_x(0, 0)
            copy_x(1, 0)
            for i in turns(act, tiles // R):
                e = expert_of(ACTE, R * i, R)
                for r in range(R):
                    act.wait_ge(s_hT[r], i + 1)
                    before(act, s_mm, r, i)
                    for m in range(HC):
                        ins = act.activation(hT[:, 0, m, :], p_t[m // 4][0:HP, (m % 4) * TT:(m % 4 + 1) * TT], func,
                                             bias=b1T[0:HP, bass.ds(e[r] * HC + m, 1)])
                    ins.then_inc(s_g[r], 1)
                    copy_x(*ahead(r, i, 2))

        @block.vector
        def _(dve):
            def copy_h(r, i):
                dve.wait_ge(s_h[r], i + 1)
                before(dve, s_hT, r, i)
                for n in range(HB):
                    ins = dve.tensor_copy(hid[:, 0, n * NW:(n + 1) * NW], p_h[n][:, 0:NW])
                ins.then_inc(s_hc[r], 1)

            if HP < 128:
                dve.memset(hid[:, 0, H:HW], 0.0).then_inc(s_wide, 1)
            copy_h(0, 0)
            for i in turns(dve, tiles // R):
                e = expert_of(DVE, R * i, R)
                for r in range(R):
                    copy_h(*ahead(r, i, 1))
                    dve.wait_ge(s_mm[r], i + 1)
                    if due(i):
                        dve.wait_ge(s_st[r], i * 16)
                    dve.tensor_tensor(y[:, r, :], p_y[:, 0:DIM], b2[:, bass.ds(e[r] * DIM, DIM)], ALU.add).then_inc(s_y[r], 1)


def first_ffn(nc, k, a):
    HC = H0 // 128
    with ExitStack() as scope:
        sb, ps, sem = new(nc, scope)
        w1 = sb("ffn0_w1", [128, KC, E0 * H0])
        w2 = sb("ffn0_w2", [128, HC, E0 * DIM])
        b1T = sb("ffn0_b1T", [128, E0 * HC])
        b2 = sb("ffn0_b2", [128, E0 * DIM])
        expert_bias(nc, k, a, w1, b1T[:, :])
        with ExitStack() as ctx:
            s_w = new(nc, ctx)[2]("s_w2ld")
            block = ctx.enter_context(nc.Block())

            @block.sync
            def _(sp):
                for m in range(HC):
                    sp.dma_start(w2[:, m, :].rearrange("p (e d) -> p e d", e=E0),
                                 a["L0_ffn_W2"].rearrange("e (m p) d -> m p e d", p=128)[m]).then_inc(s_w, 16)
                sp.dma_start(b2[:, :], rep(a["L0_ffn_b2"].rearrange("e d -> (e d)"), 128)).then_inc(s_w, 16)
                sp.wait_ge(s_w, 16 * (HC + 1))
        experts(nc, k, "f0", NT0, E0, H0, w1, w2, b1T, b2, ACT.Gelu)


def second_ffn(nc, k, a):
    with ExitStack() as scope:
        sb, ps, sem = new(nc, scope)
        w1 = sb("ffn1_w1", [128, KC, E1 * H1])
        w2 = sb("ffn1_w2", [H1, 1, E1 * DIM])
        b1r = sb("ffn1_b1r", [E1, H1])
        b1T = sb("ffn1_b1T", [H1, E1])
        b2 = sb("ffn1_b2", [128, E1 * DIM])
        with ExitStack() as ctx:
            _, ps2, _ = new(nc, ctx)
            p_b = ps2("p_b1T")
            s_w = new(nc, ctx)[2]("s_w1ld")
            s_b = new(nc, ctx)[2]("s_b1ld")
            s_T = new(nc, ctx)[2]("s_b1T")
            block = ctx.enter_context(nc.Block())

            @block.sync
            def _(sp):
                sp.dma_start(b1r[:, :], a["L1_ffn_b1"]).then_inc(s_b, 16)
                for c in range(KC):
                    sp.dma_start(w1[:, c, :].rearrange("p (e h) -> p e h", e=E1),
                                 a["L1_ffn_W1"].rearrange("e (c p) h -> c p e h", p=128)[c]).then_inc(s_w, 16)
                sp.dma_start(w2[:, 0, :].rearrange("p (e d) -> p e d", e=E1),
                             a["L1_ffn_W2"].rearrange("e p d -> p e d")).then_inc(s_w, 16)
                sp.dma_start(b2[:, :], rep(a["L1_ffn_b2"].rearrange("e d -> (e d)"), 128)).then_inc(s_w, 16)
                sp.wait_ge(s_w, 16 * (KC + 2))

            @block.tensor
            def _(pe):
                pe.wait_ge(s_b, 16)
                pe.transpose(p_b[0:H1, 0:E1], b1r[:, :], k.ident[0:E1, 0:E1]).then_inc(s_T, 1)

            @block.vector
            def _(dve):
                dve.wait_ge(s_T, 1)
                dve.tensor_copy(b1T[:, :], p_b[0:H1, 0:E1])
        experts(nc, k, "f1", NT1, E1, H1, w1, w2, b1T, b2, ACT.Relu)


def combine(nc, k, tag, table, top, out, relu=False):
    G = 8
    CH = 10
    with ExitStack() as ctx:
        sb, ps, sem = new(nc, ctx)
        got = sb("got" + tag, [B, G, top, DIM])
        s_x, s_o = sem("s_x" + tag), sem("s_o" + tag)
        s_got = [sem(f"s_got{r}_{tag}") for r in range(G)]
        s_used = sem("s_used" + tag)
        s_part = sem("s_part" + tag)
        block = ctx.enter_context(nc.Block())

        @block.sync
        def _(sp):
            issue_rows(sp, k, table, s_x)
            for t in range(CH, NB + 1, CH):
                sp.wait_ge(s_used, t)
                rows_dma(sp, out.rearrange("(t p) d -> p t d", p=B)[:, t - CH:t, :], k.X[:, t - CH:t, :], s_o)
            sp.wait_ge(s_o, 32 * (NB // CH))

        @block.gpsimd
        def _(pool):
            for t in range(NB):
                if t >= G:
                    pool.wait_ge(s_used, t - G + 1)
                for n in range(top):
                    pool.indirect_dma_start(
                        out=got[:, t % G, n, :], out_offset=None, in_=k.yg_dram,
                        in_offset=bass.IndirectOffsetOnAxis(ap=k.slot[:, n, t:t + 1], axis=0)).then_inc(s_got[t % G], 16)

        @block.vector
        def _(dve):
            dve.wait_ge(s_x, 32)
            for t in range(NB):
                x = k.X[:, t, :]
                dve.wait_ge(s_got[t % G], (t // G + 1) * 16 * top)
                if relu:
                    dve.scalar_tensor_tensor(x, got[:, t % G, 0, :], 0.0, x, ALU.max, ALU.add).then_inc(s_used, 1)
                else:
                    dve.scalar_tensor_tensor(x, got[:, t % G, 0, :], k.gate[:, 0, t:t + 1], x,
                                             ALU.mult, ALU.add).then_inc(s_part, 1)
                    dve.wait_ge(s_part, t + 1)
                    dve.scalar_tensor_tensor(x, got[:, t % G, 1, :], k.gate[:, 1, t:t + 1], x,
                                             ALU.mult, ALU.add).then_inc(s_used, 1)
                if not relu:
                    dve.wait_ge(s_used, t + 1)
                    dve.bn_stats(k.stat[:, t, :], x)


def batch_norm(nc, k, a):
    with ExitStack() as ctx:
        sb, ps, sem = new(nc, ctx)
        par = sb("bn_par", [128, 3, DIM])
        zero = sb("bn_zero", [B, DIM])
        mean = sb("bn_mean", [128, DIM])
        var, root, gain, tmp = (sb("bn_" + n, [128, DIM]) for n in ("var", "root", "gain", "tmp"))
        sq = sb("bn_sq", [B, 2, DIM])
        yv = sb("bn_y", [B, 2, DIM])
        p_m, p_v = ps("p_bnm"), ps("p_bnv")
        s_par, s_x, s_st, s_z, s_agg, s_sum, s_link, s_root, s_done = (
            sem("s_bn" + n) for n in ("par", "x", "st", "z", "agg", "sum", "link", "root", "done"))
        s_d, s_q, s_u = ([sem(f"s_bn{n}{h}") for h in range(2)] for n in ("d", "q", "u"))
        s_a, s_b = ([sem(f"s_bn{n}{h}") for h in range(2)] for n in ("a", "b"))
        block = ctx.enter_context(nc.Block())

        @block.sync
        def _(sp):
            for n, name in enumerate(("L1_gnn_bias", "L1_gnn_bn_gamma", "L1_gnn_bn_beta")):
                sp.dma_start(par[:, n, :], rep(a[name], 128)).then_inc(s_par, 16)
            issue_rows(sp, k, k.x2_dram, s_x)
            for t in range(10, NB + 1, 10):
                sp.wait_ge(s_done, t)
                rows_dma(sp, k.x3_dram.rearrange("(t p) d -> p t d", p=B)[:, t - 10:t, :], k.X[:, t - 10:t, :], s_st)
            sp.wait_ge(s_st, 32 * (NB // 10))

        @block.tensor
        def _(pe):
            pe.wait_ge(s_z, 1)
            pe.matmul(p_m[:, 0:DIM], zero[:, 0:128], zero[:, :], start=True, stop=False, skip_group_check=True)
            for t in turns(pe, NB):
                pe.wait_ge(s_agg, t + 1)
                pe.matmul(p_m[:, 0:DIM], k.ones[0:B, :], k.acc[:, bass.ds(t, 1), :].rearrange("p o d -> p (o d)"),
                          start=False, stop=False, skip_group_check=True)
            pe.matmul(p_m[:, 0:DIM], zero[:, 0:128], zero[:, :], start=False, stop=True,
                      skip_group_check=True).then_inc(s_sum, 1)
            pe.matmul(p_v[:, 0:DIM], zero[:, 0:128], zero[:, :], start=True, stop=False, skip_group_check=True)
            for i in turns(pe, NB // 2):
                for h in range(2):
                    pe.wait_ge(s_q[h], i + 1)
                    pe.matmul(p_v[:, 0:DIM], k.ones[0:B, :], sq[:, h, :], start=False, stop=False,
                              skip_group_check=True).then_inc(s_u[h], 1)
            pe.matmul(p_v[:, 0:DIM], zero[:, 0:128], zero[:, :], start=False, stop=True,
                      skip_group_check=True).then_inc(s_sum, 1)

        @block.scalar
        def _(act):
            for i in turns(act, NB // 2):
                for h in range(2):
                    act.wait_ge(s_d[h], i + 1)
                    if due(i):
                        act.wait_ge(s_u[h], i)
                    act.activation(sq[:, h, :], k.acc[:, bass.ds(2 * i + h, 1), :].rearrange("p o d -> p (o d)"),
                                   ACT.Square).then_inc(s_q[h], 1)
            act.wait_ge(s_root, 1)
            act.activation(root[:, :], var[:, :], ACT.Sqrt).then_inc(s_root, 1)

        @block.vector
        def _(dve):
            link = linker(dve, s_link)

            def row(t):
                return t[:, :, :].rearrange("p o d -> p (o d)")

            dve.memset(zero[:, :], 0.0).then_inc(s_z, 1)
            dve.wait_ge(s_par, 48)
            for t in turns(dve, NB):
                o = row(k.acc[:, bass.ds(t, 1), :])
                dve.scalar_tensor_tensor(o, o, k.norm[:, 1, bass.ds(t, 1)], par[0:B, 0, :],
                                         ALU.mult, ALU.add).then_inc(s_agg, 1)
            dve.wait_ge(s_sum, 1)
            link(dve.tensor_scalar(mean[:, :], p_m[:, 0:DIM], 1.0 / NODES, None, ALU.mult))
            for i in turns(dve, NB // 2):
                for h in range(2):
                    o = row(k.acc[:, bass.ds(2 * i + h, 1), :])
                    dve.tensor_tensor(o, o, mean[0:B, :], ALU.subtract).then_inc(s_d[h], 1)
            dve.wait_ge(s_sum, 2)
            dve.tensor_scalar(var[:, :], p_v[:, 0:DIM], 1.0 / NODES, BN_EPS, ALU.mult, ALU.add).then_inc(s_root, 1)
            dve.wait_ge(s_root, 2)
            rsqrt(link, dve, gain[:, :], var[:, :], root[:, :], tmp[:, :])
            link(dve.tensor_tensor(gain[:, :], gain[:, :], par[:, 1, :], ALU.mult))
            dve.wait_ge(s_x, 32)
            for i in turns(dve, NB // 2):
                for h in range(2):
                    dve.tensor_tensor(yv[:, h, :], row(k.acc[:, bass.ds(2 * i + h, 1), :]), gain[0:B, :],
                                      ALU.mult).then_inc(s_a[h], 1)
                for h in range(2):
                    dve.wait_ge(s_a[h], i + 1)
                    dve.tensor_tensor(yv[:, h, :], yv[:, h, :], par[0:B, 2, :], ALU.add).then_inc(s_b[h], 1)
                for h in range(2):
                    x = row(k.X[:, bass.ds(2 * i + h, 1), :])
                    dve.wait_ge(s_b[h], i + 1)
                    dve.scalar_tensor_tensor(x, yv[:, h, :], 0.0, x, ALU.max, ALU.add).then_inc(s_done, 1)
                for h in range(2):
                    dve.wait_ge(s_done, 2 * i + h + 1)
                    dve.bn_stats(row(k.stat[:, bass.ds(2 * i + h, 1), :]), row(k.X[:, bass.ds(2 * i + h, 1), :]))


def clear_slots(nc, k, a):
    with ExitStack() as ctx:
        sb, ps, sem = new(nc, ctx)
        s_z = sem("s_cz")
        block = ctx.enter_context(nc.Block())

        @block.vector
        def _(dve):
            dve.memset(k.zero[:, :], 0.0).then_inc(s_z, 1)

        @block.sync
        def _(sp):
            issue_rows(sp, k, a["x"], k.s_x)
            sp.wait_ge(s_z, 1)
            rows = (NT0 + 2) * TT
            for c in range(0, rows, 128 * 4):
                m = min(4, (rows - c) // 128)
                sp.dma_start(k.xg_dram[c:c + 128 * m, :].rearrange("(p t) d -> p (t d)", p=128),
                             k.zero[:, 0:m * DIM]).then_inc(k.s_clear, 16)
                k.clears += 16


def turn_router(nc, k, a, wr):
    with ExitStack() as ctx:
        sb, ps, sem = new(nc, ctx)
        p = ps("p_wr")
        s_l, s_T = sem("s_wrl"), sem("s_wrT")
        block = ctx.enter_context(nc.Block())

        @block.sync
        def _(sp):
            sp.dma_start(wr[:, :], a["L1_ffn_router_w"]).then_inc(s_l, 16)

        @block.tensor
        def _(pe):
            pe.wait_ge(s_l, 16)
            for c in range(KC):
                ins = pe.transpose(p[:, c * E1:(c + 1) * E1], wr[:, c * 128:(c + 1) * 128], k.ident[0:E1, 0:E1])
            ins.then_inc(s_T, 1)

        @block.vector
        def _(dve):
            dve.wait_ge(s_T, 1)
            dve.tensor_copy(k.wrT[:, :, :].rearrange("p c e -> p (c e)"), p[:, 0:KC * E1])


def build(nc, a, scratch, upto=99):
    k = Parts()
    k.blk_dram = scratch("blk_dram", (STEPS,), I32)
    k.edges = {name: scratch("edges_" + name, (NT * ET,), dt)
               for name, dt in (("src", I32), ("dst", I32), ("edge_weight", F32))}
    k.table1 = scratch("table1", (NODES, HID), F32)
    k.table2 = scratch("table2", (NODES, HID), F32)
    k.table3 = scratch("table3", (NODES, DIM), F32)
    k.x1_dram = scratch("x1", (NODES, DIM), F32)
    k.x2_dram = scratch("x2", (NODES, DIM), F32)
    k.x3_dram = scratch("x3", (NODES, DIM), F32)
    k.xg_dram = scratch("xg", ((NT0 + 2) * TT, DIM), F32)
    k.yg_dram = scratch("yg", (NT0 * TT, DIM), F32)
    with ExitStack() as ctx:
        sb, ps, sem = new(nc, ctx)
        k.iota = sb("iota", [128, 128])
        k.col = sb("col", [128, 1])
        k.ident = sb("ident", [128, 128])
        k.later = sb("later", [128, 128])
        k.ones = sb("ones", [128, 128])
        k.src_idx = sb("src_idx", [ET, SPAD], I32)
        k.dst_rel = sb("dst_rel", [ET, SPAD])
        k.weight = sb("weight", [ET, SPAD])
        k.step_blk = sb("step_blk", [1, STEPS], I32)
        k.norm = sb("norm", [B, 2, NB])
        k.stat = sb("stat", [B, NB, 6])
        k.s_x = sem("s_x_first")
        k.s_clear, k.clears = sem("s_clear"), 0
        k.zero = sb("zero", [128, 4 * DIM])
        k.slot = sb("slot", [B, TOPK, NB], I32)
        k.gate = sb("gate", [B, TOPK, NB])
        k.tile_exp = sb("tile_exp", [1, NT0 + 2], I32)
        with ExitStack() as scope:
            acc = new(nc, scope)[0]("acc", [B, NB, HID])
            k.acc = acc
            with ExitStack() as inner:
                k.X = new(nc, inner)[0]("X1", [B, NB, DIM])
                k.in_blk = new(nc, inner)[0]("in_blk", [SP, SG, NB])
                clear_slots(nc, k, a)
                schedule(nc, k, a)
                degrees(nc, k, a)
                project(nc, k, "g1", a["L0_gnn_W1"].rearrange("(c p) n -> p c n", p=128), HID, k.acc, k.norm[:, 0, :])
            store_rows(nc, "t1", k.acc[:, :, :], k.table1)
            aggregate(nc, k, "a1", k.table1, HID, k.acc, False)
            hidden(nc, k, a)
            store_rows(nc, "t2", k.acc[:, :, :], k.table2)
            aggregate(nc, k, "a2", k.table2, HID, k.acc, False)
            k.X = new(nc, scope)[0]("X2", [B, NB, DIM])
            k.logits = new(nc, scope)[0]("logits0", [B, NB, E0])
            conv_out(nc, k, a)
            project(nc, k, "r0", a["L0_ffn_Wr"].rearrange("(c p) n -> p c n", p=128), E0, k.logits, keep=True)
            renormalise(nc, k)
            route(nc, k, a, "q0", E0, TOPK, a["L0_ffn_br"], NT0)
            dispatch(nc, k, "d0", TOPK)
        if upto == 3:
            return
        first_ffn(nc, k, a)
        with ExitStack() as scope:
            k.X = new(nc, scope)[0]("X3", [B, NB, DIM])
            k.acc = new(nc, scope)[0]("acc3", [B, NB, DIM])
            combine(nc, k, "c0", k.x1_dram, TOPK, k.x2_dram)
            project(nc, k, "g3", a["L1_gnn_weight"].rearrange("(c p) n -> p c n", p=128), DIM, k.acc, k.norm[:, 1, :])
            store_rows(nc, "t3", k.acc[:, :, :], k.table3)
            aggregate(nc, k, "a3", k.table3, DIM, k.acc, True)
            batch_norm(nc, k, a)
            k.logits = new(nc, scope)[0]("logits1", [B, NB, E1])
            with ExitStack() as inner:
                wr = new(nc, inner)[0]("wr_rows", [E1, DIM])
                k.wrT = new(nc, inner)[0]("wrT", [128, KC, E1])
                turn_router(nc, k, a, wr)
                project(nc, k, "r1", None, E1, k.logits, keep=True)
            route(nc, k, a, "q1", E1, 1, a["L1_ffn_router_b"], NT1)
            dispatch(nc, k, "d1", 1)
        second_ffn(nc, k, a)
        with ExitStack() as scope:
            k.X = new(nc, scope)[0]("X4", [B, NB, DIM])
            combine(nc, k, "c1", k.x3_dram, 1, a["out"], relu=True)


_INS = ["x", "src", "dst", "edge_weight", "L0_gnn_W1", "L0_gnn_b1", "L0_gnn_W2", "L0_gnn_b2", "L0_ffn_Wr", "L0_ffn_br",
        "L0_ffn_ln_g", "L0_ffn_ln_b", "L0_ffn_W1", "L0_ffn_b1", "L0_ffn_W2", "L0_ffn_b2", "L1_gnn_weight",
        "L1_gnn_bias", "L1_gnn_bn_gamma", "L1_gnn_bn_beta", "L1_ffn_router_w", "L1_ffn_router_b", "L1_ffn_W1",
        "L1_ffn_b1", "L1_ffn_W2", "L1_ffn_b2"]


def kernel(**inputs):
    import numpy as _np
    import concourse.bacc as _bacc
    from concourse.bass_utils import run_bass_kernel_spmd as _run

    nc = _bacc.Bacc("TRN2", target_bir_lowering=False, num_devices=1)
    arrays, a = {}, {}
    for name in _INS:
        arrays[name] = _np.ascontiguousarray(inputs[name])
        a[name] = nc.dram_tensor(name, arrays[name].shape, mybir.dt.from_np(arrays[name].dtype),
                                 kind="ExternalInput").ap()
    a["out"] = nc.dram_tensor("out", (NODES, DIM), F32, kind="ExternalOutput").ap()
    build(nc, a, lambda name, shape, dt: nc.dram_tensor(name, shape, dt).ap())
    return _run(nc, [arrays], core_ids=[0]).results[0]["out"]
```
